# Optimizing a Trainium2 kernel written in Bass

```python
import numpy as np
import jax
import jax.numpy as jnp

def _softmax(x, axis=-1):
    return jax.nn.softmax(x, axis=axis)

def _gelu(x):
    return jax.nn.gelu(x, approximate=True)

def _silu(x):
    return jax.nn.silu(x)

def _sigmoid(x):
    return jax.nn.sigmoid(x)

def _layernorm(x, axis=-1, eps=1e-05):
    m = jnp.mean(x, axis=axis, keepdims=True)
    v = jnp.var(x, axis=axis, keepdims=True)
    return (x - m) / jnp.sqrt(v + eps)

def _scatter_add(tgt, idx, src, axis=0):
    return tgt.at[idx].add(src)

def _segment_sum(src, seg, n):
    return jax.ops.segment_sum(src, seg, n)
kernel_name = 'mk_hybrid_d2_jaxref_r8_7d5246'

def setup_inputs(seed: int=0):
    np.random.seed(seed)
    _w = jnp.asarray

    def _L0_attn_a_setup():
        import jax, jax.numpy as jnp
        import numpy as np
        HEADS = 16
        key = jax.random.key(seed)
        ks = jax.random.split(key, 5)
        B, T, D = (2, 256, 256)
        s = 0.02
        return {'x': jax.random.normal(ks[0], (B, T, D), dtype=jnp.float32), 'Wq': jax.random.normal(ks[1], (D, D), dtype=jnp.float32) * s, 'Wk': jax.random.normal(ks[2], (D, D), dtype=jnp.float32) * s, 'Wv': jax.random.normal(ks[3], (D, D), dtype=jnp.float32) * s, 'Wo': jax.random.normal(ks[4], (D, D), dtype=jnp.float32) * s}
    _L0_attn_a_in = _L0_attn_a_setup()

    def _L0_attn_b_setup():
        import jax, jax.numpy as jnp
        import numpy as np
        from jax import lax
        B, T, D_MODEL = (4, 256, 256)
        EXPAND, D_CONV = (2, 4)
        D_INNER = D_MODEL * EXPAND

        def _forward(x, w_in, w_out, conv_w, conv_b, D):
            x_proj = jnp.einsum('btc,dc->btd', x, w_in)
            xi, gate = jnp.split(x_proj, 2, axis=-1)
            xc = jnp.transpose(xi, (0, 2, 1))
            xc = lax.conv_general_dilated(xc, conv_w, window_strides=(1,), padding=[(D_CONV - 1, 0)], dimension_numbers=('NCH', 'OIH', 'NCH'), feature_group_count=D_INNER) + conv_b[None, :, None]
            xc = jnp.transpose(xc, (0, 2, 1))
            h = jax.nn.silu(xc) * D[None, None, :] * jax.nn.silu(gate)
            return jnp.einsum('btd,cd->btc', h, w_out)
        key = jax.random.key(seed)
        ks = jax.random.split(key, 5)
        x = jax.random.normal(ks[0], (B, T, D_MODEL), dtype=jnp.float32)
        w_in = jax.random.normal(ks[1], (2 * D_INNER, D_MODEL), dtype=jnp.float32) * D_MODEL ** (-0.5)
        w_out = jax.random.normal(ks[2], (D_MODEL, D_INNER), dtype=jnp.float32) * D_INNER ** (-0.5)
        conv_w = jax.random.normal(ks[3], (D_INNER, 1, D_CONV), dtype=jnp.float32) * D_CONV ** (-0.5)
        conv_b = jax.random.normal(ks[4], (D_INNER,), dtype=jnp.float32) * 0.02
        D = jnp.ones((D_INNER,), dtype=jnp.float32)
        return {'x': x, 'w_in': w_in, 'w_out': w_out, 'conv_w': conv_w, 'conv_b': conv_b, 'D': D}
    _L0_attn_b_in = _L0_attn_b_setup()

    def _L0_ffn_setup():
        import jax, jax.numpy as jnp
        import numpy as np
        B, S, D = (2, 256, 256)
        E = 8
        TOPK = 2
        H_SHARED = 1024
        H_ROUTED = 128
        STD = 0.02
        key = jax.random.key(seed)
        ks = jax.random.split(key, 7)
        return {'x': jax.random.normal(ks[0], (B, S, D), jnp.float32), 'w12': jax.random.normal(ks[1], (E, 2 * H_ROUTED, D), jnp.float32) * STD, 'w3': jax.random.normal(ks[2], (E, D, H_ROUTED), jnp.float32) * STD, 'router_w': jax.random.normal(ks[3], (E, D), jnp.float32) * STD, 'expert_bias': jnp.zeros((E,), jnp.float32), 'sw1': jax.random.normal(ks[4], (H_SHARED, D), jnp.float32) * STD, 'sw2': jax.random.normal(ks[5], (H_SHARED, D), jnp.float32) * STD, 'sw3': jax.random.normal(ks[6], (D, H_SHARED), jnp.float32) * STD}
    _L0_ffn_in = _L0_ffn_setup()

    def _L1_attn_a_setup():
        import jax, jax.numpy as jnp
        import numpy as np
        D_INNER, D_STATE, DT_RANK = (256, 16, 128)
        BATCH, SEQ = (2, 256)

        def _selective_scan(u, delta, A, B, C, D):
            dA = jnp.exp(delta[..., None] * A[None, None])
            dBu = (delta * u)[..., None] * B[:, :, None, :]

            def step(h, inp):
                dA_t, dBu_t, C_t = inp
                h = dA_t * h + dBu_t
                y_t = jnp.einsum('bdn,bn->bd', h, C_t)
                return (h, y_t)
            h0 = jnp.zeros((u.shape[0], u.shape[2], A.shape[1]), dtype=u.dtype)
            xs = (jnp.moveaxis(dA, 1, 0), jnp.moveaxis(dBu, 1, 0), jnp.moveaxis(C, 1, 0))
            _, ys = jax.lax.scan(step, h0, xs)
            y = jnp.moveaxis(ys, 0, 1)
            return y + u * D[None, None, :]
        key = jax.random.key(seed)
        ks = jax.random.split(key, 6)
        x = jax.random.normal(ks[0], (BATCH, SEQ, D_INNER), dtype=jnp.float32)
        A_log = jax.random.uniform(ks[1], (D_INNER, D_STATE), minval=-4.0, maxval=-1.0, dtype=jnp.float32)
        D = jnp.ones((D_INNER,), dtype=jnp.float32)
        x_proj_w = jax.random.normal(ks[2], (DT_RANK + 2 * D_STATE, D_INNER), dtype=jnp.float32) / np.sqrt(D_INNER)
        dt_proj_w = jax.random.normal(ks[3], (D_INNER, DT_RANK), dtype=jnp.float32) / np.sqrt(DT_RANK)
        dt_std = DT_RANK ** (-0.5)
        dt_proj_b = jax.random.uniform(ks[4], (D_INNER,), minval=-dt_std, maxval=dt_std, dtype=jnp.float32)
        return {'x': x, 'A_log': A_log, 'D': D, 'x_proj_w': x_proj_w, 'dt_proj_w': dt_proj_w, 'dt_proj_b': dt_proj_b}
    _L1_attn_a_in = _L1_attn_a_setup()

    def _L1_attn_b_setup():
        import jax, jax.numpy as jnp
        import numpy as np
        B, S, HID = (2, 256, 256)
        NH, NKV, HD = (32, 4, 128)
        EPS = 1e-06
        ROPE_THETA = 1000000.0

        def _rms_norm(x, w):
            xf = x.astype(jnp.float32)
            var = jnp.mean(xf * xf, axis=-1, keepdims=True)
            return (w * (xf * jax.lax.rsqrt(var + EPS))).astype(x.dtype)

        def _rope_tables(seq_len, head_dim, dtype):
            inv_freq = 1.0 / ROPE_THETA ** (jnp.arange(0, head_dim, 2, dtype=jnp.float32) / head_dim)
            t = jnp.arange(seq_len, dtype=jnp.float32)
            freqs = jnp.outer(t, inv_freq)
            emb = jnp.concatenate([freqs, freqs], axis=-1)
            return (jnp.cos(emb).astype(dtype), jnp.sin(emb).astype(dtype))

        def _rotate_half(x):
            x1, x2 = jnp.split(x, 2, axis=-1)
            return jnp.concatenate([-x2, x1], axis=-1)

        def _apply_rope(q, k, cos, sin):
            cos = cos[None, None, :, :]
            sin = sin[None, None, :, :]
            q = q * cos + _rotate_half(q) * sin
            k = k * cos + _rotate_half(k) * sin
            return (q, k)
        key = jax.random.key(seed)
        ks = jax.random.split(key, 7)
        s = 0.02
        return {'hidden_states': jax.random.normal(ks[0], (B, S, HID), jnp.float32), 'Wq': jax.random.normal(ks[1], (HID, NH * HD), jnp.float32) * s, 'Wk': jax.random.normal(ks[2], (HID, NKV * HD), jnp.float32) * s, 'Wv': jax.random.normal(ks[3], (HID, NKV * HD), jnp.float32) * s, 'Wo': jax.random.normal(ks[4], (NH * HD, HID), jnp.float32) * s, 'q_norm_w': jnp.ones((HD,), jnp.float32), 'k_norm_w': jnp.ones((HD,), jnp.float32)}
    _L1_attn_b_in = _L1_attn_b_setup()

    def _L1_ffn_setup():
        import jax, jax.numpy as jnp
        import numpy as np
        H = 256
        I = 128
        E = 16
        K = 2
        B, S = (4, 128)
        key = jax.random.key(seed)
        ks = jax.random.split(key, 5)
        scale = 0.02
        x = jax.random.normal(ks[0], (B, S, H), dtype=jnp.float32)
        gate_w = jax.random.normal(ks[1], (E, H), dtype=jnp.float32) * scale
        wg = jax.random.normal(ks[2], (E, H, I), dtype=jnp.float32) * scale
        wu = jax.random.normal(ks[3], (E, H, I), dtype=jnp.float32) * scale
        wd = jax.random.normal(ks[4], (E, I, H), dtype=jnp.float32) * scale
        return {'x': x, 'gate_w': gate_w, 'wg': wg, 'wu': wu, 'wd': wd}
    _L1_ffn_in = _L1_ffn_setup()
    _d = {'L0_attn_a_x': _L0_attn_a_in['x'], 'L0_attn_a_Wq': _L0_attn_a_in['Wq'], 'L0_attn_a_Wk': _L0_attn_a_in['Wk'], 'L0_attn_a_Wv': _L0_attn_a_in['Wv'], 'L0_attn_a_Wo': _L0_attn_a_in['Wo'], 'L0_attn_b_w_in': _L0_attn_b_in['w_in'], 'L0_attn_b_w_out': _L0_attn_b_in['w_out'], 'L0_attn_b_conv_w': _L0_attn_b_in['conv_w'], 'L0_attn_b_conv_b': _L0_attn_b_in['conv_b'], 'L0_attn_b_D': _L0_attn_b_in['D'], 'L0_ffn_w12': _L0_ffn_in['w12'], 'L0_ffn_w3': _L0_ffn_in['w3'], 'L0_ffn_router_w': _L0_ffn_in['router_w'], 'L0_ffn_expert_bias': _L0_ffn_in['expert_bias'], 'L0_ffn_sw1': _L0_ffn_in['sw1'], 'L0_ffn_sw2': _L0_ffn_in['sw2'], 'L0_ffn_sw3': _L0_ffn_in['sw3'], 'L1_attn_a_A_log': _L1_attn_a_in['A_log'], 'L1_attn_a_D': _L1_attn_a_in['D'], 'L1_attn_a_x_proj_w': _L1_attn_a_in['x_proj_w'], 'L1_attn_a_dt_proj_w': _L1_attn_a_in['dt_proj_w'], 'L1_attn_a_dt_proj_b': _L1_attn_a_in['dt_proj_b'], 'L1_attn_b_Wq': _L1_attn_b_in['Wq'], 'L1_attn_b_Wk': _L1_attn_b_in['Wk'], 'L1_attn_b_Wv': _L1_attn_b_in['Wv'], 'L1_attn_b_Wo': _L1_attn_b_in['Wo'], 'L1_attn_b_q_norm_w': _L1_attn_b_in['q_norm_w'], 'L1_attn_b_k_norm_w': _L1_attn_b_in['k_norm_w'], 'L1_ffn_gate_w': _L1_ffn_in['gate_w'], 'L1_ffn_wg': _L1_ffn_in['wg'], 'L1_ffn_wu': _L1_ffn_in['wu'], 'L1_ffn_wd': _L1_ffn_in['wd']}
    _x0 = _d['L0_attn_a_x']
    _d['L0_attn_a_x'] = jax.random.normal(jax.random.fold_in(jax.random.key(seed), 1), (1, 1024, 256), dtype=_x0.dtype)
    del _x0
    return _d

def reference(L0_attn_a_x, L0_attn_a_Wq, L0_attn_a_Wk, L0_attn_a_Wv, L0_attn_a_Wo, L0_attn_b_w_in, L0_attn_b_w_out, L0_attn_b_conv_w, L0_attn_b_conv_b, L0_attn_b_D, L0_ffn_w12, L0_ffn_w3, L0_ffn_router_w, L0_ffn_expert_bias, L0_ffn_sw1, L0_ffn_sw2, L0_ffn_sw3, L1_attn_a_A_log, L1_attn_a_D, L1_attn_a_x_proj_w, L1_attn_a_dt_proj_w, L1_attn_a_dt_proj_b, L1_attn_b_Wq, L1_attn_b_Wk, L1_attn_b_Wv, L1_attn_b_Wo, L1_attn_b_q_norm_w, L1_attn_b_k_norm_w, L1_ffn_gate_w, L1_ffn_wg, L1_ffn_wu, L1_ffn_wd):

    def _L0_attn_a_ref(x, Wq, Wk, Wv, Wo):
        import jax, jax.numpy as jnp
        import numpy as np
        HEADS = 16
        B, T, _ = x.shape
        H = HEADS
        Dh = Wq.shape[1] // H
        q = (x @ Wq).reshape(B, T, H, Dh)
        k = (x @ Wk).reshape(B, T, H, Dh)
        v = (x @ Wv).reshape(B, T, H, Dh)
        scores = jnp.einsum('bthd,bshd->bhts', q, k)
        mask = jnp.tril(jnp.ones((T, T), dtype=scores.dtype))
        scores = scores * mask
        attn = jax.nn.softmax(scores / T ** 0.5, axis=-1)
        out = jnp.einsum('bhts,bshd->bthd', attn, v).reshape(B, T, H * Dh)
        return out @ Wo

    def _L0_attn_b_ref(x, w_in, w_out, conv_w, conv_b, D):
        import jax, jax.numpy as jnp
        import numpy as np
        from jax import lax
        B, T, D_MODEL = (4, 256, 256)
        EXPAND, D_CONV = (2, 4)
        D_INNER = D_MODEL * EXPAND

        def _forward(x, w_in, w_out, conv_w, conv_b, D):
            x_proj = jnp.einsum('btc,dc->btd', x, w_in)
            xi, gate = jnp.split(x_proj, 2, axis=-1)
            xc = jnp.transpose(xi, (0, 2, 1))
            xc = lax.conv_general_dilated(xc, conv_w, window_strides=(1,), padding=[(D_CONV - 1, 0)], dimension_numbers=('NCH', 'OIH', 'NCH'), feature_group_count=D_INNER) + conv_b[None, :, None]
            xc = jnp.transpose(xc, (0, 2, 1))
            h = jax.nn.silu(xc) * D[None, None, :] * jax.nn.silu(gate)
            return jnp.einsum('btd,cd->btc', h, w_out)
        return _forward(x, w_in, w_out, conv_w, conv_b, D)

    def _L0_ffn_ref(x, w12, w3, router_w, expert_bias, sw1, sw2, sw3):
        import jax, jax.numpy as jnp
        import numpy as np
        B, S, D = (2, 256, 256)
        E = 8
        TOPK = 2
        H_SHARED = 1024
        H_ROUTED = 128
        STD = 0.02
        b, s, d = x.shape
        g = x @ sw1.T
        u = x @ sw2.T
        shared_out = jax.nn.silu(g) * u @ sw3.T
        scores = jax.nn.sigmoid(x @ router_w.T)
        selection_scores = scores + expert_bias
        _, top_idx = jax.lax.top_k(selection_scores, TOPK)
        top_scores = jnp.take_along_axis(scores, top_idx, axis=-1)
        top_scores = top_scores / (top_scores.sum(-1, keepdims=True) + 1e-09)
        flat_x = x.reshape(-1, d)
        T = flat_x.shape[0]
        flat_idx = top_idx.reshape(T, TOPK)
        flat_sc = top_scores.reshape(T, TOPK)
        combine = jnp.zeros((T, E), x.dtype).at[jnp.arange(T)[:, None], flat_idx].add(flat_sc)
        h12 = jnp.einsum('td,ehd->teh', flat_x, w12)
        h1, h2 = jnp.split(h12, 2, axis=-1)
        h = jax.nn.silu(h1) * h2
        out_e = jnp.einsum('teh,edh->ted', h, w3)
        routed_out = jnp.einsum('ted,te->td', out_e, combine).reshape(b, s, d)
        return shared_out + routed_out

    def _L1_attn_a_ref(x, A_log, D, x_proj_w, dt_proj_w, dt_proj_b):
        import jax, jax.numpy as jnp
        import numpy as np
        D_INNER, D_STATE, DT_RANK = (256, 16, 128)
        BATCH, SEQ = (2, 256)

        def _selective_scan(u, delta, A, B, C, D):
            dA = jnp.exp(delta[..., None] * A[None, None])
            dBu = (delta * u)[..., None] * B[:, :, None, :]

            def step(h, inp):
                dA_t, dBu_t, C_t = inp
                h = dA_t * h + dBu_t
                y_t = jnp.einsum('bdn,bn->bd', h, C_t)
                return (h, y_t)
            h0 = jnp.zeros((u.shape[0], u.shape[2], A.shape[1]), dtype=u.dtype)
            xs = (jnp.moveaxis(dA, 1, 0), jnp.moveaxis(dBu, 1, 0), jnp.moveaxis(C, 1, 0))
            _, ys = jax.lax.scan(step, h0, xs)
            y = jnp.moveaxis(ys, 0, 1)
            return y + u * D[None, None, :]
        x_dbl = jnp.einsum('bld,ed->ble', x, x_proj_w)
        delta_r = x_dbl[..., :DT_RANK]
        B = x_dbl[..., DT_RANK:DT_RANK + D_STATE]
        C = x_dbl[..., DT_RANK + D_STATE:]
        delta = jnp.einsum('blr,dr->bld', delta_r, dt_proj_w) + dt_proj_b
        delta = jax.nn.softplus(delta)
        A = -jnp.exp(A_log)
        return _selective_scan(x, delta, A, B, C, D)

    def _L1_attn_b_ref(hidden_states, Wq, Wk, Wv, Wo, q_norm_w, k_norm_w):
        import jax, jax.numpy as jnp
        import numpy as np
        B, S, HID = (2, 256, 256)
        NH, NKV, HD = (32, 4, 128)
        EPS = 1e-06
        ROPE_THETA = 1000000.0

        def _rms_norm(x, w):
            xf = x.astype(jnp.float32)
            var = jnp.mean(xf * xf, axis=-1, keepdims=True)
            return (w * (xf * jax.lax.rsqrt(var + EPS))).astype(x.dtype)

        def _rope_tables(seq_len, head_dim, dtype):
            inv_freq = 1.0 / ROPE_THETA ** (jnp.arange(0, head_dim, 2, dtype=jnp.float32) / head_dim)
            t = jnp.arange(seq_len, dtype=jnp.float32)
            freqs = jnp.outer(t, inv_freq)
            emb = jnp.concatenate([freqs, freqs], axis=-1)
            return (jnp.cos(emb).astype(dtype), jnp.sin(emb).astype(dtype))

        def _rotate_half(x):
            x1, x2 = jnp.split(x, 2, axis=-1)
            return jnp.concatenate([-x2, x1], axis=-1)

        def _apply_rope(q, k, cos, sin):
            cos = cos[None, None, :, :]
            sin = sin[None, None, :, :]
            q = q * cos + _rotate_half(q) * sin
            k = k * cos + _rotate_half(k) * sin
            return (q, k)
        b, s, _ = hidden_states.shape
        scaling = HD ** (-0.5)
        q = (hidden_states @ Wq).reshape(b, s, NH, HD)
        k = (hidden_states @ Wk).reshape(b, s, NKV, HD)
        v = (hidden_states @ Wv).reshape(b, s, NKV, HD)
        q = _rms_norm(q, q_norm_w)
        k = _rms_norm(k, k_norm_w)
        q = jnp.transpose(q, (0, 2, 1, 3))
        k = jnp.transpose(k, (0, 2, 1, 3))
        v = jnp.transpose(v, (0, 2, 1, 3))
        cos, sin = _rope_tables(s, HD, q.dtype)
        q, k = _apply_rope(q, k, cos, sin)
        groups = NH // NKV
        k = jnp.repeat(k, groups, axis=1)
        v = jnp.repeat(v, groups, axis=1)
        scores = jnp.einsum('bhqd,bhkd->bhqk', q, k) * scaling
        causal = jnp.tril(jnp.ones((s, s), bool))
        scores = jnp.where(causal[None, None], scores, jnp.finfo(scores.dtype).min)
        attn = jax.nn.softmax(scores.astype(jnp.float32), axis=-1).astype(q.dtype)
        out = jnp.einsum('bhqk,bhkd->bhqd', attn, v)
        out = jnp.transpose(out, (0, 2, 1, 3)).reshape(b, s, NH * HD)
        return out @ Wo

    def _L1_ffn_ref(x, gate_w, wg, wu, wd):
        import jax, jax.numpy as jnp
        import numpy as np
        H = 256
        I = 128
        E = 16
        K = 2
        B, S = (4, 128)
        b, s, h = x.shape
        xf = x.reshape(-1, h)
        T = xf.shape[0]
        scores = jax.nn.softmax(xf @ gate_w.T, axis=-1)
        topk_w, topk_idx = jax.lax.top_k(scores, K)
        topk_w = topk_w / (jnp.sum(topk_w, axis=-1, keepdims=True) + 1e-20)
        combine = jnp.zeros((T, E), dtype=xf.dtype).at[jnp.arange(T)[:, None], topk_idx].add(topk_w)
        g = jnp.einsum('th,ehi->tei', xf, wg)
        u = jnp.einsum('th,ehi->tei', xf, wu)
        a = jax.nn.silu(g) * u * combine[:, :, None]
        y = jnp.einsum('tei,eih->th', a, wd)
        return y.reshape(b, s, h)
    x = L0_attn_a_x
    x = x + _L0_attn_a_ref(_layernorm(x, axis=-1), L0_attn_a_Wq, L0_attn_a_Wk, L0_attn_a_Wv, L0_attn_a_Wo)
    x = x + _L0_ffn_ref(_layernorm(x, axis=-1), L0_ffn_w12, L0_ffn_w3, L0_ffn_router_w, L0_ffn_expert_bias, L0_ffn_sw1, L0_ffn_sw2, L0_ffn_sw3)
    x = x + _L0_attn_b_ref(_layernorm(x, axis=-1), L0_attn_b_w_in, L0_attn_b_w_out, L0_attn_b_conv_w, L0_attn_b_conv_b, L0_attn_b_D)
    x = x + _L0_ffn_ref(_layernorm(x, axis=-1), L0_ffn_w12, L0_ffn_w3, L0_ffn_router_w, L0_ffn_expert_bias, L0_ffn_sw1, L0_ffn_sw2, L0_ffn_sw3)
    x = x + _L1_attn_a_ref(_layernorm(x, axis=-1), L1_attn_a_A_log, L1_attn_a_D, L1_attn_a_x_proj_w, L1_attn_a_dt_proj_w, L1_attn_a_dt_proj_b)
    x = x + _L1_ffn_ref(_layernorm(x, axis=-1), L1_ffn_gate_w, L1_ffn_wg, L1_ffn_wu, L1_ffn_wd)
    x = x + _L1_attn_b_ref(_layernorm(x, axis=-1), L1_attn_b_Wq, L1_attn_b_Wk, L1_attn_b_Wv, L1_attn_b_Wo, L1_attn_b_q_norm_w, L1_attn_b_k_norm_w)
    x = x + _L1_ffn_ref(_layernorm(x, axis=-1), L1_ffn_gate_w, L1_ffn_wg, L1_ffn_wu, L1_ffn_wd)
    return x

_drawn_inputs = setup_inputs


def setup_inputs(seed=0):
    import zlib

    import numpy as np

    out = dict(_drawn_inputs(seed))
    spreads = {'L0_attn_b_D': (1.0, 0.2),
     'L0_ffn_expert_bias': (0.0, 0.1),
     'L1_attn_a_D': (1.0, 0.6),
     'L1_attn_b_q_norm_w': (1.0, 0.6),
     'L1_attn_b_k_norm_w': (1.0, 0.6)}
    factors = {'L0_attn_a_Wq': 8.0,
     'L0_attn_a_Wk': 8.0,
     'L0_attn_a_Wv': 8.0,
     'L0_attn_a_Wo': 8.0,
     'L0_attn_b_conv_b': 4.069,
     'L0_ffn_router_w': 2.695,
     'L1_attn_a_dt_proj_b': 2.925,
     'L1_attn_b_Wq': 8.0,
     'L1_attn_b_Wk': 8.0,
     'L1_attn_b_Wv': 8.0,
     'L1_attn_b_Wo': 8.0,
     'L1_ffn_gate_w': 8.0,
     'L1_ffn_wg': 8.0,
     'L1_ffn_wu': 8.0,
     'L1_ffn_wd': 8.0}
    for name, (base, spread) in spreads.items():
        noise = np.random.default_rng([zlib.crc32(name.encode()), seed]).standard_normal(out[name].shape)
        drawn = base * np.exp(spread * noise) if base else spread * noise
        out[name] = jnp.asarray(drawn.astype(out[name].dtype))
    for name, factor in factors.items():
        out[name] = (out[name] * factor).astype(out[name].dtype)
    return out
```

```python
from contextlib import ExitStack

import concourse.bass as bass
from concourse import mybir

F32 = mybir.dt.float32
BF16 = mybir.dt.bfloat16
ALU = mybir.AluOpType
ACT = mybir.ActivationFunctionType
AX = mybir.AxisListType.X

P = 128
T, D = 1024, 256
NT = T // P
DC = D // P
HALF = 512
LN_EPS = 1e-5
E = 16
BIG = 1e30


class Steps:

    def __init__(self, eng, sem):
        self.eng, self.sem, self.n = eng, sem, 0

    def then(self, ins):
        self.n += 1
        ins.then_inc(self.sem, 1)
        self.eng.wait_ge(self.sem, self.n)


class Sems:

    def __init__(self, nc, tag):
        self.nc, self.tag, self.all = nc, tag, []

    def __enter__(self):
        return self

    def __call__(self, name):
        self.all.append(self.nc.alloc_semaphore(f"{self.tag}_{name}"))
        return self.all[-1]

    def __exit__(self, *_):
        self.nc.clear_and_free_semaphores(self.all)
        self.nc.all_engine_barrier()


class Core:

    def __init__(self, nc, ctx):
        def sb(name, shape, dt=F32):
            return ctx.enter_context(nc.sbuf_tensor(name, shape, dt))

        self.nc = nc
        self.x = sb("stream", [P, NT, D])
        self.xnT = sb("xnT", [P, DC, T])
        self.ident = sb("ident", [P, P])
        self.zeros = sb("zeros", [P, HALF], BF16)
        self.minus_half = sb("minus_half", [P, NT])
        self.acc = ctx.enter_context(nc.psum_tensor("acc", [P, 4, HALF], F32))
        self.aux = ctx.enter_context(nc.psum_tensor("aux", [P, 4, HALF], F32))


def constants(nc, core, x_dram):
    with ExitStack() as ctx:
        sem = ctx.enter_context(Sems(nc, "start"))
        x_in = sem("x_in")
        filled = sem("filled")
        block = ctx.enter_context(nc.Block())

        @block.sync
        def _(sp):
            sp.dma_start(core.x[:, :, :], x_dram.rearrange("(n p) d -> p n d", p=P)).then_inc(x_in, 16)
            sp.wait_ge(x_in, 16)

        @block.gpsimd
        def _(pool):
            pool.memset(core.ident[:, :], 0.0).then_inc(filled, 1)
            pool.wait_ge(filled, 1)
            pool.affine_select(out=core.ident[:, :], in_=core.ident[:, :], compare_op=ALU.not_equal,
                               fill=1.0, base=0, pattern=[[-1, P]], channel_multiplier=1)
            pool.memset(core.zeros[:, :], 0.0)
            pool.memset(core.minus_half[:, :], -0.5)


class Norm:

    def __init__(self, nc, core, ctx, sem, tag):
        def sb(name, shape, dt=F32):
            return ctx.enter_context(nc.sbuf_tensor(f"{tag}_{name}", shape, dt))

        self.core = core
        self.stats = sb("ln_stats", [P, NT, 6])
        self.mv = sb("ln_mean_var", [P, NT, 2])
        self.rstd = sb("ln_rstd", [P, NT])
        self.xn = sb("ln_xn", [P, NT, D])
        self.stats_done = sem("stats_done")
        self.var_ready = sem("var_ready")
        self.eps_added = sem("eps_added")
        self.rstd_ready = sem("rstd_ready")
        self.xn_ready = sem("xn_ready")
        self.turned = sem("turned")
        self.xnT_ready = sem("xnT_ready")

    def vector(self, dve):
        c = self.core
        for t in range(NT):
            dve.bn_stats(self.stats[:, t, :], c.x[:, t, :]).then_inc(self.stats_done, 1)
        for t in range(NT):
            dve.wait_ge(self.stats_done, t + 1)
            dve.bn_aggr(self.mv[:, t, :], self.stats[:, t, :]).then_inc(self.var_ready, 1)
        dve.wait_ge(self.rstd_ready, 1)
        for t in range(NT):
            dve.tensor_scalar(self.xn[:, t, :], c.x[:, t, :], self.mv[:, t, 0:1], self.rstd[:, t:t + 1],
                              ALU.subtract, ALU.mult).then_inc(self.xn_ready, 1)

    def gpsimd(self, pool):
        pool.wait_ge(self.var_ready, NT)
        pool.tensor_scalar(self.rstd[:, :], self.mv[:, :, 1], LN_EPS, None, ALU.add).then_inc(self.eps_added, 1)
        pool.wait_ge(self.eps_added, 1)
        pool.tensor_tensor(self.rstd[:, :], self.rstd[:, :], self.core.minus_half[:, :],
                           ALU.pow).then_inc(self.rstd_ready, 1)

    def tensor(self, pe):
        c = self.core
        for q in range(NT // 2):
            pe.wait_ge(self.xn_ready, 2 * q + 2)
            for t in (2 * q, 2 * q + 1):
                for k in range(DC):
                    last = pe.transpose(c.acc[:, q, (2 * k + t % 2) * P:(2 * k + t % 2 + 1) * P],
                                        self.xn[:, t, k * P:(k + 1) * P], c.ident[:, :])
            last.then_inc(self.turned, 1)

    def scalar(self, act):
        c = self.core
        for q in range(NT // 2):
            act.wait_ge(self.turned, q + 1)
            act.activation(c.xnT[:, :, 2 * q * P:(2 * q + 2) * P],
                           c.acc[:, q, :].rearrange("p (k t) -> p k t", k=DC),
                           ACT.Copy).then_inc(self.xnT_ready, 1)


def ffn_layer(nc, core, tag, up_dram, down_dram, router_dram, bias_dram, comb_dram, shared):
    routed = E - shared
    with ExitStack() as ctx:
        def sb(name, shape, dt=F32):
            return ctx.enter_context(nc.sbuf_tensor(f"{tag}_{name}", shape, dt))

        sem = ctx.enter_context(Sems(nc, tag))
        norm = Norm(nc, core, ctx, sem, tag)
        w_up = sb("w_up", [P, 2, DC, 2 * P])
        w_down = sb("w_down", [P, 2, D])
        silu_g = sb("silu_g", [P, 2, HALF])
        hidden = sb("hidden", [P, 2, HALF])
        weighted = sb("weighted", [P, 2, HALF])
        comb_all = sb("comb_all", [P, 2, T])
        w_router = sb("w_router", [P, DC, routed])
        bias = sb("bias", [P, routed])
        probs = sb("probs", [P, NT, routed])
        select = sb("select", [P, NT, routed])
        rank = sb("rank", [P, NT, routed])
        falling = sb("falling", [P, NT, routed])
        first = sb("first", [P, NT, routed])
        second = sb("second", [P, NT, routed])
        comb = sb("comb", [P, NT, E])
        stat = sb("stat", [P, NT])
        combT = sb("combT", [E, T])

        router_in = sem("router_in")
        iota_done = sem("iota_done")
        logits_ready = sem("logits_ready")
        shifted = sem("shifted")
        exp_ready = sem("exp_ready")
        comb_ready = sem("comb_ready")
        combT_turned = sem("combT_turned")
        combT_ready = sem("combT_ready")
        comb_stored = sem("comb_stored")
        comb_in = [sem("comb_in0"), sem("comb_in1")]
        up_in = [sem("up_in0"), sem("up_in1")]
        down_in = [sem("down_in0"), sem("down_in1")]
        g_ready = sem("g_ready")
        u_ready = sem("u_ready")
        silu_ready = sem("silu_ready")
        hidden_ready = sem("hidden_ready")
        weighted_ready = sem("weighted_ready")
        down_done = sem("down_done")
        small = sem("small")
        added = sem("added")
        acc, aux = core.acc, core.aux
        block = ctx.enter_context(nc.Block())

        @block.sync
        def _(sp):
            sp.dma_start(w_router[:, :, :], router_dram).then_inc(router_in, 16)
            if bias_dram is not None:
                sp.dma_start(bias[:, :], bias_dram.rearrange("(a e) -> a e", a=1).to_broadcast([P, routed])).then_inc(router_in, 16)
            for s in range(2):
                sp.dma_start(w_up[:, s], up_dram[s]).then_inc(up_in[s], 16)
                sp.dma_start(w_down[:, s], down_dram[s]).then_inc(down_in[s], 16)
            sp.wait_ge(combT_ready, 2)
            sp.dma_start(comb_dram, combT[:, :]).then_inc(comb_stored, 16)
            sp.wait_ge(comb_stored, 16)
            for s in range(2):
                sp.dma_start(comb_all[:, s, :], comb_dram[s:s + 1, :].to_broadcast([P, T])).then_inc(comb_in[s], 16)
            with sp.Fori(1, E // 2) as i:
                for s in range(2):
                    e = 2 * i + s
                    sp.wait_ge(down_done, 4 * i + 2 * s)
                    sp.dma_start(comb_all[:, s, :], comb_dram[bass.ds(e, 1), :].to_broadcast([P, T])).then_inc(comb_in[s], 16)
                    sp.dma_start(w_up[:, s], up_dram[bass.ds(e, 1)].rearrange("a p k n -> (a p) k n")).then_inc(up_in[s], 16)
                    sp.dma_start(w_down[:, s], down_dram[bass.ds(e, 1)].rearrange("a p n -> (a p) n")).then_inc(down_in[s], 16)

        @block.gpsimd
        def _(pool):
            for t in range(NT):
                pool.iota(falling[:, t, :], [[-1, routed]], base=routed, channel_multiplier=0,
                          allow_small_or_imprecise_dtypes=True).then_inc(iota_done, 1)
            if shared:
                pool.memset(comb[:, :, routed:], 1.0).then_inc(iota_done, 1)
            norm.gpsimd(pool)

            def weigh(i, s):
                e = 2 * i + s
                pool.wait_ge(comb_in[s], 16 * i + 16)
                for h in range(2):
                    n = 2 * e + h
                    pool.wait_ge(hidden_ready, n + 1)
                    pool.wait_ge(down_done, n + 1)
                    pool.tensor_tensor(weighted[:, h], hidden[:, h], comb_all[:, s, h * HALF:(h + 1) * HALF],
                                       ALU.mult).then_inc(weighted_ready, 1)

            with pool.Fori(0, E // 2) as i:
                for s in range(2):
                    weigh(i, s)

        @block.scalar
        def _(act):
            norm.scalar(act)
            act.wait_ge(logits_ready, 1)
            if shared:
                act.activation(select[:, :, :], acc[:, 0, 0:NT * routed].rearrange("p (t e) -> p t e", e=routed),
                               ACT.Exp, scale=-1.0).then_inc(exp_ready, 1)
            else:
                act.wait_ge(shifted, 1)
                act.activation(probs[:, :, :], select[:, :, :], ACT.Exp).then_inc(exp_ready, 1)
            for h in range(2):
                act.wait_ge(combT_turned, 4 * h + 4)
                act.activation(combT[:, h * HALF:(h + 1) * HALF], acc[0:E, 1 + h, :], ACT.Copy).then_inc(combT_ready, 1)
            with act.Fori(0, E // 2) as i:
                for j in range(4):
                    act.wait_ge(g_ready, 4 * i + j + 1)
                    act.activation(silu_g[:, j % 2], aux[:, j % 2 * 2, :], ACT.Silu).then_inc(silu_ready, 1)

        @block.vector
        def _(dve):
            norm.vector(dve)
            s = Steps(dve, small)
            wide = [P, NT, routed]

            def over(stat_ap):
                return stat_ap.unsqueeze(2).to_broadcast(wide)

            logits = acc[:, 0, 0:NT * routed].rearrange("p (t e) -> p t e", e=routed)
            if shared:
                dve.wait_ge(exp_ready, 1)
                s.then(dve.tensor_scalar(select[:], select[:], 1.0, None, ALU.add))
                s.then(dve.reciprocal(probs[:], select[:]))
                dve.wait_ge(router_in, 32)
                s.then(dve.tensor_tensor(select[:], probs[:], bias[:, :].unsqueeze(1).to_broadcast(wide), ALU.add))
            else:
                dve.wait_ge(logits_ready, 1)
                s.then(dve.tensor_reduce(stat[:], logits, AX, ALU.max))
                dve.tensor_tensor(select[:], logits, over(stat[:]), ALU.subtract).then_inc(shifted, 1)
                dve.wait_ge(exp_ready, 1)
                s.then(dve.tensor_reduce(stat[:], probs[:], AX, ALU.add))
                s.then(dve.reciprocal(stat[:], stat[:]))
                s.then(dve.tensor_tensor(probs[:], probs[:], over(stat[:]), ALU.mult))
                s.then(dve.tensor_copy(select[:], probs[:]))
            dve.wait_ge(iota_done, NT + (1 if shared else 0))
            for best in (first, second):
                s.then(dve.tensor_reduce(stat[:], select[:], AX, ALU.max))
                s.then(dve.tensor_tensor(rank[:], select[:], over(stat[:]), ALU.is_equal))
                s.then(dve.tensor_tensor(rank[:], rank[:], falling[:], ALU.mult))
                s.then(dve.tensor_reduce(stat[:], rank[:], AX, ALU.max))
                s.then(dve.tensor_tensor(best[:], rank[:], over(stat[:]), ALU.is_equal))
                if best is first:
                    s.then(dve.scalar_tensor_tensor(select[:], first[:], -BIG, select[:], ALU.mult, ALU.add))
            s.then(dve.tensor_tensor(first[:], first[:], second[:], ALU.add))
            s.then(dve.tensor_tensor(first[:], first[:], probs[:], ALU.mult))
            s.then(dve.tensor_reduce(stat[:], first[:], AX, ALU.add))
            s.then(dve.tensor_scalar(stat[:], stat[:], 1e-9 if shared else 1e-20, None, ALU.add))
            s.then(dve.reciprocal(stat[:], stat[:]))
            dve.tensor_tensor(comb[:, :, 0:routed], first[:], over(stat[:]), ALU.mult).then_inc(comb_ready, 1)

            with dve.Fori(0, E // 2) as i:
                for j in range(4):
                    n = 4 * i + j
                    dve.wait_ge(silu_ready, n + 1)
                    dve.wait_ge(u_ready, n + 1)
                    dve.tensor_tensor(hidden[:, j % 2], silu_g[:, j % 2], aux[:, j % 2 * 2 + 1, :],
                                      ALU.mult).then_inc(hidden_ready, 1)
            dve.wait_ge(down_done, 2 * E + 2)
            for q in range(4):
                dve.tensor_tensor(core.x[:, 2 * q:2 * q + 2, :], core.x[:, 2 * q:2 * q + 2, :],
                                  acc[:, q, :].rearrange("p (t d) -> p t d", t=2), ALU.add).then_inc(added, 1)

        @block.tensor
        def _(pe):
            norm.tensor(pe)
            pe.wait_ge(norm.xnT_ready, NT // 2)
            pe.wait_ge(router_in, 32 if bias_dram is not None else 16)
            for t in range(NT):
                for k in range(DC):
                    last = pe.matmul(acc[:, 0, t * routed:(t + 1) * routed], core.xnT[:, k, t * P:(t + 1) * P],
                                     w_router[:, k, :], start=(k == 0), stop=(k == DC - 1))
            last.then_inc(logits_ready, 1)

            def up(i, j):
                n = 4 * i + j
                b = j % 2
                s = j // 2 % 2
                if j % 2 == 0:
                    pe.wait_ge(up_in[s], 16 * (i + j // 4) + 16)
                for w, ready in ((0, g_ready), (1, u_ready)):
                    for k in range(DC):
                        last = pe.matmul(aux[:, 2 * b + w, :], w_up[:, s, k, w * P:(w + 1) * P],
                                         core.xnT[:, k, b * HALF:(b + 1) * HALF],
                                         start=(k == 0), stop=(k == DC - 1))
                    last.then_inc(ready, 1)

            def down(i, j):
                n = 4 * i + j
                s = j // 2
                if j % 2 == 0:
                    pe.wait_ge(down_in[s], 16 * i + 16)
                pe.wait_ge(weighted_ready, n + 1)
                for t in range(NT // 2):
                    tile = (j % 2) * (NT // 2) + t
                    last = pe.matmul(acc[:, tile // 2, tile % 2 * D:(tile % 2 + 1) * D],
                                     weighted[:, j % 2, t * P:(t + 1) * P], w_down[:, s, :],
                                     start=False, stop=False, skip_group_check=True)
                last.then_inc(down_done, 1)

            up(0, 0)
            up(0, 1)
            pe.wait_ge(comb_ready, 1)
            for t in range(NT):
                pe.transpose(acc[0:E, 1 + t // 4, t % 4 * P:(t % 4 + 1) * P], comb[:, t, :],
                             core.ident[:, :]).then_inc(combT_turned, 1)
            pe.wait_ge(combT_ready, 2)
            for q in range(4):
                last = pe.matmul(acc[:, q, :], core.zeros[:, 0:P], core.zeros[:, :], start=True, stop=True,
                                 skip_group_check=True)
            last.then_inc(down_done, 2)

            with pe.Fori(0, E // 2 - 1) as i:
                for j in range(4):
                    down(i, j)
                    up(i, j + 2)
            last_i = E // 2 - 1
            for j in range(2):
                down(last_i, j)
                up(last_i, j + 2)
            for j in range(2, 4):
                down(last_i, j)


HEADS, KV, HD = 32, 4, 128
GQ = HEADS // KV
STEPS = GQ * NT
TILE_ORDER = [0, 7, 1, 6, 2, 5, 3, 4]
RMS_EPS = 1e-6


def gqa_layer(nc, core, wq_dram, wk_dram, wv_dram, wo_dram, norm_w_dram, cos_dram, sin_dram):
    with ExitStack() as ctx:
        def sb(name, shape, dt=F32):
            return ctx.enter_context(nc.sbuf_tensor(f"gqa_{name}", shape, dt))

        sem = ctx.enter_context(Sems(nc, "gqa"))
        norm = Norm(nc, core, ctx, sem, "gqa")
        wq = sb("wq", [P, DC, GQ * HD])
        wk = sb("wk", [P, DC, HD])
        wv = sb("wv", [P, DC, HD])
        wo = sb("wo", [P, GQ, D])
        cos_w = [sb("cos_k", [P, T]), sb("cos_q", [P, T])]
        sin_w = [sb("sin_k", [P, T]), sb("sin_q", [P, T])]
        norm_w = sb("norm_w", [P, 2])
        eps = sb("eps", [P, 2])
        ones = sb("ones", [P, P])
        below = sb("below", [P, P], BF16)
        ident_b = sb("ident_b", [P, P], BF16)
        square = sb("square", [P, 2, T])
        straight = sb("straight", [P, 2, T])
        turned_q = sb("turned_q", [P, 2, T])
        rms = sb("rms", [P, 2, T])
        kT = sb("kT", [P, T])
        v = sb("v", [P, NT, HD])
        qT = sb("qT", [P, GQ, T])
        q_now = sb("q_now", [P, 2, T])
        probs = sb("probs", [P, 4, T])
        probsT = sb("probsT", [P, 4, T])
        neg_max = sb("neg_max", [P, 16])
        row_sum = sb("row_sum", [P, 16])
        row_inv = sb("row_inv", [P, 16])
        oT = sb("oT", [P, GQ, T])

        tables_in = sem("tables_in")
        norm_w_in = sem("norm_w_in")
        made = sem("made")
        consts = sem("consts")
        tables_ready = sem("tables_ready")
        qkv_w_in = sem("qkv_w_in")
        wo_in = sem("wo_in")
        v_done = sem("v_done")
        v_ready = sem("v_ready")
        projected = sem("projected")
        squared = sem("squared")
        roped = sem("roped")
        rope_summed = sem("rope_summed")
        square_sum = sem("square_sum")
        logged = sem("logged")
        rms_ready = sem("rms_ready")
        qk_ready = sem("qk_ready")
        q_in = [sem("q_in0"), sem("q_in1")]
        scored = sem("scored")
        max_ready = sem("max_ready")
        exp_done = sem("exp_done")
        inv_ready = sem("inv_ready")
        scaled = sem("scaled")
        chunk_turned = sem("chunk_turned")
        chunk_copied = sem("chunk_copied")
        pv_done = sem("pv_done")
        oT_copied = sem("oT_copied")
        wo_done = sem("wo_done")
        added = sem("added")
        acc, aux = core.acc, core.aux
        ITEMS = 1 + GQ

        def chunks(j):
            def of(t):
                return t // 4 + 1
            before = sum(of(TILE_ORDER[m % NT]) for m in range(j % NT)) + j // NT * 12
            return before, of(TILE_ORDER[j % NT])

        def steady(eng, stages):
            lead = max(lag for lag, _ in stages) + 2
            for n in range(lead):
                for lag, stage in stages:
                    if n >= lag:
                        stage(0, n - lag)
            rounds = (STEPS - lead) // 16
            with eng.Fori(0, rounds) as i:
                for j in range(lead, lead + 16):
                    for lag, stage in stages:
                        stage(i, j - lag)
            for j in range(lead, STEPS - 16 * rounds + lead):
                for lag, stage in stages:
                    if j - lag < STEPS - 16 * rounds:
                        stage(rounds, j - lag)

        block = ctx.enter_context(nc.Block())

        @block.sync
        def _(sp):
            def load(g):
                sp.dma_start(wq[:, :, :], wq_dram[bass.ds(g, 1)].rearrange("a p k n -> (a p) k n")).then_inc(qkv_w_in, 16)
                sp.dma_start(wk[:, :, :], wk_dram[bass.ds(g, 1)].rearrange("a p k n -> (a p) k n")).then_inc(qkv_w_in, 16)
                sp.dma_start(wv[:, :, :], wv_dram[bass.ds(g, 1)].rearrange("a p k n -> (a p) k n")).then_inc(qkv_w_in, 16)

            def load_wo(g):
                sp.dma_start(wo[:, :, :], wo_dram[bass.ds(g, 1)].rearrange("a p h n -> (a p) h n")).then_inc(wo_in, 16)

            sp.dma_start(norm_w[:, :], norm_w_dram).then_inc(norm_w_in, 16)
            sp.dma_start(probs[:, 0, :], cos_dram).then_inc(tables_in, 16)
            sp.dma_start(probs[:, 1, :], sin_dram).then_inc(tables_in, 16)
            load(0)
            load_wo(0)

            def copy(i, s):
                sp.dma_start(q_now[:, s, :], qT[:, bass.ds(2 * i + s, 1), :].rearrange("p a t -> p (a t)")).then_inc(q_in[s], 16)

            def group(g):
                sp.wait_ge(qk_ready, ITEMS * g + 2)
                copy(0, 0)
                sp.wait_ge(qk_ready, ITEMS * g + ITEMS)
                copy(0, 1)
                with sp.Fori(1, GQ // 2) as i:
                    for s in range(2):
                        sp.wait_ge(scored, STEPS * g + 16 * i + 8 * s - 8)
                        copy(i, s)

            with sp.Fori(0, KV - 1) as g:
                group(g)
                load(g + 1)
                sp.wait_ge(wo_done, NT * g + NT)
                load_wo(g + 1)
            group(KV - 1)

        @block.gpsimd
        def _(pool):
            norm.gpsimd(pool)
            pool.memset(eps[:, 0:1], RMS_EPS).then_inc(made, 1)
            pool.memset(eps[:, 1:2], RMS_EPS * HD).then_inc(made, 1)
            pool.memset(ones[:, :], 1.0).then_inc(made, 1)
            pool.memset(below[:, :], 0.0).then_inc(made, 1)
            pool.wait_ge(made, 4)
            pool.affine_select(out=below[:, :], in_=below[:, :], compare_op=ALU.is_ge, fill=-BIG,
                               base=0, pattern=[[-1, P]], channel_multiplier=1).then_inc(made, 1)
            pool.tensor_copy(ident_b[:, :], core.ident[:, :]).then_inc(made, 1)

            def group(g):
                for m in range(ITEMS):
                    pool.wait_ge(roped, ITEMS * g + m + 1)
                    pool.tensor_tensor(straight[:, m % 2], straight[:, m % 2], turned_q[:, m % 2],
                                       ALU.add).then_inc(rope_summed, 1)


            with pool.Fori(0, KV) as g:
                group(g)

        @block.scalar
        def _(act):
            norm.scalar(act)

            def group(g):
                for h in range(2):
                    act.wait_ge(v_done, 2 * g + h + 1)
                    act.activation(v[:, 4 * h:4 * h + 4, :], aux[:, 2 + h, :].rearrange("p (t d) -> p t d", d=HD),
                                   ACT.Copy).then_inc(v_ready, 1)
                for m in range(ITEMS + 1):
                    if m < ITEMS:
                        act.wait_ge(projected, ITEMS * g + m + 1)
                        act.activation(square[:, m % 2], acc[:, 2 * (m % 2):2 * (m % 2) + 2, :].rearrange("p a b -> p (a b)"),
                                       ACT.Square).then_inc(squared, 1)
                    if m >= 1:
                        r = m - 1
                        kind = 0 if r == 0 else 1
                        act.wait_ge(square_sum, ITEMS * g + r + 1)
                        if r >= 2:
                            act.wait_ge(qk_ready, ITEMS * g + r - 1)
                        act.activation(rms[:, r % 2], aux[:, 0:2, :].rearrange("p a b -> p (a b)"), ACT.Ln,
                                       bias=eps[:, kind:kind + 1], scale=1.0 / HD if kind == 0 else 1.0).then_inc(logged, 1)
                        act.wait_ge(logged, ITEMS * g + r + 1)
                        act.activation(rms[:, r % 2], rms[:, r % 2], ACT.Exp, scale=-0.5).then_inc(rms_ready, 1)

                def exp(i, j):
                    n = STEPS * g + 16 * i + j
                    w = (TILE_ORDER[j % NT] + 1) * P
                    act.wait_ge(max_ready, n + 1)
                    act.activation(probs[:, j % 4, 0:w],
                                   acc[:, 2 * (j % 2):2 * (j % 2) + 2, :].rearrange("p a b -> p (a b)")[:, 0:w],
                                   ACT.Exp, bias=neg_max[:, j % 16:j % 16 + 1],
                                   accum_out=row_sum[:, j % 16:j % 16 + 1]).then_inc(exp_done, 1)

                def copy_out(i, j):
                    n = STEPS * g + 16 * i + j
                    t = TILE_ORDER[j % NT]
                    act.wait_ge(pv_done, n + 1)
                    act.activation(oT[:, bass.ds(2 * i + j // NT, 1), t * P:(t + 1) * P].rearrange("p a t -> p (a t)"),
                                   aux[:, 2 + j % 2, 0:P], ACT.Copy).then_inc(oT_copied, 1)

                steady(act, [(0, exp), (4, copy_out)])

            with act.Fori(0, KV) as g:
                group(g)

        @block.vector
        def _(dve):
            norm.vector(dve)
            dve.wait_ge(norm_w_in, 16)
            dve.wait_ge(tables_in, 32)
            for kind in range(2):
                dve.tensor_scalar(cos_w[kind][:, :], probs[:, 0, :], norm_w[:, kind:kind + 1], None, ALU.mult).then_inc(tables_ready, 1)
                dve.tensor_scalar(sin_w[kind][0:64, :], probs[0:64, 1, :], norm_w[0:64, kind:kind + 1], None, ALU.mult).then_inc(tables_ready, 1)
                dve.tensor_scalar(sin_w[kind][64:128, :], probs[64:128, 1, :], norm_w[64:128, kind:kind + 1], -1.0,
                                  ALU.mult, ALU.mult).then_inc(tables_ready, 1)
            dve.wait_ge(tables_ready, 6)

            def group(g):
                for m in range(ITEMS + 1):
                    if m < ITEMS:
                        kind = 0 if m == 0 else 1
                        src = acc[:, 2 * (m % 2):2 * (m % 2) + 2, :].rearrange("p a b -> p (a b)")
                        dve.wait_ge(squared, ITEMS * g + m + 1)
                        if m >= 2:
                            dve.wait_ge(qk_ready, ITEMS * g + m - 1)
                        dve.tensor_tensor(straight[:, m % 2], src, cos_w[kind][:, :], ALU.mult)
                        dve.tensor_tensor(turned_q[0:64, m % 2], src[64:128], sin_w[kind][64:128, :], ALU.mult)
                        dve.tensor_tensor(turned_q[64:128, m % 2], src[0:64], sin_w[kind][0:64, :], ALU.mult).then_inc(roped, 1)
                    if m >= 1:
                        r = m - 1
                        dve.wait_ge(rms_ready, ITEMS * g + r + 1)
                        dve.wait_ge(rope_summed, ITEMS * g + r + 1)
                        out = kT[:, :] if r == 0 else qT[:, r - 1, :]
                        dve.tensor_tensor(out, straight[:, r % 2], rms[:, r % 2], ALU.mult).then_inc(qk_ready, 1)

                def row_max(i, j):
                    n = STEPS * g + 16 * i + j
                    w = (TILE_ORDER[j % NT] + 1) * P
                    dve.wait_ge(scored, n + 1)
                    dve.tensor_reduce(neg_max[:, j % 16:j % 16 + 1],
                                      acc[:, 2 * (j % 2):2 * (j % 2) + 2, :].rearrange("p a b -> p (a b)")[:, 0:w],
                                      AX, ALU.max, negate=True).then_inc(max_ready, 1)

                def normalise(i, j):
                    n = STEPS * g + 16 * i + j
                    dve.wait_ge(exp_done, n + 1)
                    dve.reciprocal(row_inv[:, j % 16:j % 16 + 1], row_sum[:, j % 16:j % 16 + 1]).then_inc(inv_ready, 1)
                    dve.wait_ge(inv_ready, n + 1)
                    w = (TILE_ORDER[j % NT] + 1) * P
                    dve.tensor_scalar(probs[:, j % 4, 0:w], probs[:, j % 4, 0:w], row_inv[:, j % 16:j % 16 + 1],
                                      None, ALU.mult).then_inc(scaled, 1)

                def copy_chunks(i, j):
                    before, count = chunks(j)
                    w = (TILE_ORDER[j % NT] + 1) * P
                    for c in range(count):
                        k = 12 * GQ * g + 24 * i + before + c
                        dve.wait_ge(chunk_turned, k + 1)
                        a, b = c * HALF, min(w, (c + 1) * HALF)
                        dve.tensor_copy(probsT[:, j % 4, a:b], aux[:, (before + c) % 2, 0:b - a]).then_inc(chunk_copied, 1)

                steady(dve, [(0, row_max), (1, normalise), (2, copy_chunks)])
                for t in range(NT):
                    dve.wait_ge(wo_done, NT * g + t + 1)
                    dve.tensor_tensor(core.x[:, t, :], core.x[:, t, :], acc[:, t % 4, 0:D], ALU.add).then_inc(added, 1)

            with dve.Fori(0, KV) as g:
                group(g)

        @block.tensor
        def _(pe):
            norm.tensor(pe)
            pe.wait_ge(norm.xnT_ready, NT // 2)
            pe.wait_ge(made, 6)

            def group(g):
                pe.wait_ge(qkv_w_in, 48 * g + 48)
                for t in range(NT):
                    for k in range(DC):
                        last = pe.matmul(aux[:, 2 + t // 4, t % 4 * HD:(t % 4 + 1) * HD],
                                         core.xnT[:, k, t * P:(t + 1) * P], wv[:, k, :],
                                         start=(k == 0), stop=(k == DC - 1))
                    if t % 4 == 3:
                        last.then_inc(v_done, 1)
                for m in range(ITEMS + 1):
                    if m < ITEMS:
                        w = wk[:, :, :] if m == 0 else wq[:, :, (m - 1) * HD:m * HD]
                        if m >= 2:
                            pe.wait_ge(roped, ITEMS * g + m - 1)
                        for h in range(2):
                            for k in range(DC):
                                last = pe.matmul(acc[:, 2 * (m % 2) + h, :], w[:, k, :],
                                                 core.xnT[:, k, h * HALF:(h + 1) * HALF],
                                                 start=(k == 0), stop=(k == DC - 1))
                        last.then_inc(projected, 1)
                    if m >= 1:
                        r = m - 1
                        pe.wait_ge(squared, ITEMS * g + r + 1)
                        if r >= 1:
                            pe.wait_ge(logged, ITEMS * g + r)
                        for h in range(2):
                            last = pe.matmul(aux[:, h, :], ones[:, :], square[:, r % 2, h * HALF:(h + 1) * HALF],
                                             start=True, stop=True)
                        last.then_inc(square_sum, 1)

                def score(i, j):
                    n = STEPS * g + 16 * i + j
                    t = TILE_ORDER[j % NT]
                    w = (t + 1) * P
                    if j % NT == 0:
                        s = j // NT % 2
                        pe.wait_ge(q_in[s], 64 * g + 16 * i + 16 * (j // 16) + 16)
                    if isinstance(i, int) and i == 0 and j < 2:
                        pe.wait_ge(roped, ITEMS * g + ITEMS)
                        pe.wait_ge(qk_ready, ITEMS * g + 1)
                    else:
                        pe.wait_ge(exp_done, n - 1)
                    for c in range(t // 4 + 1):
                        a, b = c * HALF, min(w, (c + 1) * HALF)
                        diagonal = b == w
                        last = pe.matmul(acc[:, 2 * (j % 2) + c, 0:b - a], q_now[:, j // NT % 2, t * P:(t + 1) * P],
                                         kT[:, a:b], start=True, stop=not diagonal)
                    last = pe.matmul(acc[:, 2 * (j % 2) + c, b - a - P:b - a], ident_b[:, :], below[:, :],
                                     start=False, stop=True)
                    last.then_inc(scored, 1)

                def turn(i, j):
                    n = STEPS * g + 16 * i + j
                    before, count = chunks(j)
                    t = TILE_ORDER[j % NT]
                    pe.wait_ge(scaled, n + 1)
                    for c in range(count):
                        k = 12 * GQ * g + 24 * i + before + c
                        if isinstance(i, int) and i == 0 and before + c < 2:
                            pe.wait_ge(logged, ITEMS * g + ITEMS)
                        else:
                            pe.wait_ge(chunk_copied, k - 1)
                        for s in range(4 * c, min(t + 1, 4 * c + 4)):
                            last = pe.transpose(aux[:, (before + c) % 2, s % 4 * P:(s % 4 + 1) * P],
                                                probs[:, j % 4, s * P:(s + 1) * P], core.ident[:, :])
                        last.then_inc(chunk_turned, 1)

                def weigh(i, j):
                    n = STEPS * g + 16 * i + j
                    before, count = chunks(j)
                    t = TILE_ORDER[j % NT]
                    if isinstance(i, int) and i == 0 and j < 2:
                        pe.wait_ge(v_ready, 2 * g + 2)
                    else:
                        pe.wait_ge(oT_copied, n - 1)
                    pe.wait_ge(chunk_copied, 12 * GQ * g + 24 * i + before + count)
                    for s in range(t + 1):
                        last = pe.matmul(aux[:, 2 + j % 2, 0:P], v[:, s, :], probsT[:, j % 4, s * P:(s + 1) * P],
                                         start=(s == 0), stop=(s == t))
                    last.then_inc(pv_done, 1)

                steady(pe, [(0, score), (2, turn), (4, weigh)])
                pe.wait_ge(wo_in, 16 * g + 16)
                pe.wait_ge(oT_copied, STEPS * g + STEPS)
                for t in range(NT):
                    if t >= 4:
                        pe.wait_ge(added, NT * g + t - 3)
                    for h in range(GQ):
                        last = pe.matmul(acc[:, t % 4, 0:D], oT[:, h, t * P:(t + 1) * P], wo[:, h, :],
                                         start=(h == 0), stop=(h == GQ - 1))
                    last.then_inc(wo_done, 1)
                pe.wait_ge(added, NT * g + NT)

            with pe.Fori(0, KV) as g:
                group(g)


H0, HD0, G0 = 16, 16, 4
PAD0 = P // G0
STEPS0 = G0 * NT


def masked_attention_layer(nc, core, wq_dram, wk_dram, wv_dram, wo_dram):
    SCALE = 1.0 / T ** 0.5
    with ExitStack() as ctx:
        def sb(name, shape, dt=F32):
            return ctx.enter_context(nc.sbuf_tensor(f"mat_{name}", shape, dt))

        sem = ctx.enter_context(Sems(nc, "mat"))
        norm = Norm(nc, core, ctx, sem, "mat")
        wqk = sb("wqk", [P, 2, DC, 2 * P])
        wv = sb("wv", [P, DC, D])
        wo = sb("wo", [P, DC, D])
        ones = sb("ones", [P, P])
        after = sb("after", [P, P])
        below = sb("below", [P, P], BF16)
        ident_b = sb("ident_b", [P, P], BF16)
        top = sb("top", [P, NT])
        masked_keys = sb("masked_keys", [P, NT])
        v = sb("v", [P, NT, D])
        v_later = sb("v_later", [P, NT, D])
        v_masked = sb("v_masked", [P, NT, D])
        qk = sb("qk", [P, 2, T])
        probs = sb("probs", [P, 4, T])
        probsT = sb("probsT", [P, 4, T])
        neg_max = sb("neg_max", [P, 16])
        bias = sb("bias", [P, NT, H0])
        row_sum = sb("row_sum", [P, NT, H0])
        out = sb("out", [P, NT, H0, HD0])
        outT = sb("outT", [P, DC, T])

        made = sem("made")
        wqk_in = [sem("wqk_in0"), sem("wqk_in1")]
        wv_in = sem("wv_in")
        wo_in = sem("wo_in")
        v_done = sem("v_done")
        v_ready = sem("v_ready")
        later_ready = sem("later_ready")
        v_masked_done = sem("v_masked_done")
        v_masked_ready = sem("v_masked_ready")
        projected = sem("projected")
        qk_ready = sem("qk_ready")
        scored = sem("scored")
        max_ready = sem("max_ready")
        bias_ready = sem("bias_ready")
        exp_done = sem("exp_done")
        chunk_turned = sem("chunk_turned")
        chunk_copied = sem("chunk_copied")
        pv_done = sem("pv_done")
        out_copied = sem("out_copied")
        weight_ready = sem("weight_ready")
        small = sem("small")
        out_ready = sem("out_ready")
        out_turned = sem("out_turned")
        outT_ready = sem("outT_ready")
        wo_done = sem("wo_done")
        added = sem("added")
        acc, aux = core.acc, core.aux

        def tile_of(j):
            return TILE_ORDER[j // G0 % NT]

        def chunks(j):
            return sum(tile_of(m) // 4 + 1 for m in range(j % STEPS0)), tile_of(j) // 4 + 1

        CHUNKS = 12 * G0

        def steady(stages):
            for n in range(STEPS0 + max(lag for lag, _ in stages)):
                for lag, stage in stages:
                    if 0 <= n - lag < STEPS0:
                        stage(n - lag)

        block = ctx.enter_context(nc.Block())

        @block.sync
        def _(sp):
            sp.dma_start(wv[:, :, :], wv_dram).then_inc(wv_in, 16)
            for s in range(2):
                for w, w_dram in ((0, wq_dram), (1, wk_dram)):
                    sp.dma_start(wqk[:, s, :, w * P:(w + 1) * P], w_dram[s]).then_inc(wqk_in[s], 16)
            sp.dma_start(wo[:, :, :], wo_dram).then_inc(wo_in, 16)
            sp.wait_ge(projected, 2)
            for s in range(2):
                sp.wait_ge(projected, 2 * s + 2)
                for w, w_dram in ((0, wq_dram), (1, wk_dram)):
                    sp.dma_start(wqk[:, s, :, w * P:(w + 1) * P], w_dram[2 + s]).then_inc(wqk_in[s], 16)

        @block.gpsimd
        def _(pool):
            pool.memset(ones[:, :], 1.0).then_inc(made, 1)
            pool.memset(after[:, :], 0.0).then_inc(made, 1)
            pool.memset(below[:, :], 0.0).then_inc(made, 1)
            pool.memset(top[:, :], 0.0).then_inc(made, 1)
            pool.iota(masked_keys[:, :], [[-P, NT]], base=T - 1, channel_multiplier=-1,
                      allow_small_or_imprecise_dtypes=True).then_inc(made, 1)
            pool.tensor_copy(ident_b[:, :], core.ident[:, :]).then_inc(made, 1)
            norm.gpsimd(pool)
            pool.wait_ge(made, 6)
            pool.affine_select(out=after[:, :], in_=after[:, :], compare_op=ALU.is_ge, fill=1.0,
                               base=0, pattern=[[1, P]], channel_multiplier=-1).then_inc(made, 1)
            pool.affine_select(out=below[:, :], in_=below[:, :], compare_op=ALU.is_ge, fill=-BIG,
                               base=0, pattern=[[-1, P]], channel_multiplier=1).then_inc(made, 1)
            pool.affine_select(out=top[:, :], in_=top[:, :], compare_op=ALU.not_equal, fill=BIG,
                               base=-(T - 1), pattern=[[P, NT]], channel_multiplier=1).then_inc(made, 1)
            pool.memset(v_later[:, NT - 1, :], 0.0).then_inc(later_ready, 1)
            for t in range(NT - 2, -1, -1):
                pool.wait_ge(v_ready, 4)
                pool.wait_ge(later_ready, NT - 1 - t)
                pool.tensor_tensor(v_later[:, t, :], v_later[:, t + 1, :], v[:, t + 1, :], ALU.add).then_inc(later_ready, 1)

        @block.scalar
        def _(act):
            norm.scalar(act)
            for q in range(4):
                act.wait_ge(v_done, q + 1)
                act.activation(v[:, 2 * q:2 * q + 2, :], aux[:, q, :].rearrange("p (t d) -> p t d", t=2),
                               ACT.Copy).then_inc(v_ready, 1)

            def group(g):
                for w in range(2):
                    act.wait_ge(projected, 2 * g + w + 1)
                    act.activation(qk[:, w, :], acc[:, 2 * w:2 * w + 2, :].rearrange("p a b -> p (a b)"),
                                   ACT.Copy).then_inc(qk_ready, 1)

                def exp(j):
                    n = STEPS0 * g + j
                    t = tile_of(j)
                    w = (t + 1) * P
                    act.wait_ge(bias_ready, n + 1)
                    act.activation(probs[:, j % 4, 0:w],
                                   acc[:, 2 * (j % 2):2 * (j % 2) + 2, :].rearrange("p a b -> p (a b)")[:, 0:w],
                                   ACT.Exp, bias=bias[:, t, bass.ds(G0 * g + j % G0, 1)], scale=SCALE,
                                   accum_out=row_sum[:, t, bass.ds(G0 * g + j % G0, 1)]).then_inc(exp_done, 1)

                def copy_out(j):
                    if j % G0 == G0 - 1:
                        act.wait_ge(pv_done, 8 * g + j // G0 + 1)
                        act.activation(out[:, tile_of(j), bass.ds(G0 * g, G0), :],
                                       aux[:, 2 + j // G0 % 2, 0:G0 * HD0].rearrange("p (h d) -> p h d", d=HD0),
                                       ACT.Copy).then_inc(out_copied, 1)

                def copy_second(j):
                    before, count = chunks(j)
                    if count == 2:
                        k = CHUNKS * g + before + 1
                        act.wait_ge(chunk_turned, k + 1)
                        act.wait_ge(chunk_copied, k)
                        act.activation(probsT[:, j % 4, HALF:(tile_of(j) + 1) * P],
                                       aux[:, (before + 1) % 2, 0:(tile_of(j) + 1) * P - HALF], ACT.Copy).then_inc(chunk_copied, 1)

                steady([(0, exp), (2, copy_second), (4, copy_out)])

            with act.Fori(0, H0 // G0) as g:
                group(g)
            act.wait_ge(weight_ready, 1)
            act.activation(bias[:, :, :], bias[:, :, :], ACT.Exp).then_inc(weight_ready, 1)
            for q in range(4):
                act.wait_ge(out_turned, q + 1)
                act.activation(outT[:, :, 2 * q * P:(2 * q + 2) * P],
                               acc[:, q, :].rearrange("p (k t) -> p k t", k=DC), ACT.Copy).then_inc(outT_ready, 1)

        @block.vector
        def _(dve):
            norm.vector(dve)
            dve.wait_ge(made, 9)
            for q in range(4):
                dve.wait_ge(v_masked_done, q + 1)
                dve.tensor_copy(v_masked[:, 2 * q:2 * q + 2, :], acc[:, q, :].rearrange("p (t d) -> p t d", t=2)).then_inc(v_masked_ready, 1)

            def group(g):
                def row_max(j):
                    n = STEPS0 * g + j
                    t = tile_of(j)
                    dve.wait_ge(scored, n + 1)
                    dve.tensor_reduce(neg_max[:, j % 16:j % 16 + 1],
                                      acc[:, 2 * (j % 2):2 * (j % 2) + 2, :].rearrange("p a b -> p (a b)")[:, 0:(t + 1) * P],
                                      AX, ALU.max, negate=True).then_inc(max_ready, 1)
                    dve.wait_ge(max_ready, n + 1)
                    dve.tensor_scalar(bias[:, t, bass.ds(G0 * g + j % G0, 1)], neg_max[:, j % 16:j % 16 + 1],
                                      top[:, t:t + 1], SCALE, ALU.min, ALU.mult).then_inc(bias_ready, 1)

                def copy_first(j):
                    before, count = chunks(j)
                    k = CHUNKS * g + before
                    dve.wait_ge(chunk_turned, k + 1)
                    if j > 0:
                        dve.wait_ge(chunk_copied, k)
                    w = min(HALF, (tile_of(j) + 1) * P)
                    dve.tensor_copy(probsT[:, j % 4, 0:w], aux[:, before % 2, 0:w]).then_inc(chunk_copied, 1)

                steady([(0, row_max), (2, copy_first)])

            with dve.Fori(0, H0 // G0) as g:
                group(g)
            s = Steps(dve, small)
            dve.wait_ge(exp_done, STEPS0 * (H0 // G0))
            dve.tensor_scalar(bias[:, :, :], bias[:, :, :], 0.0, None, ALU.min).then_inc(weight_ready, 1)
            dve.wait_ge(weight_ready, 2)
            wide = [P, NT, H0, HD0]
            v_m = v_masked[:, :, :].rearrange("p t (h d) -> p t h d", d=HD0)
            for t in range(NT):
                one = [P, H0, HD0]
                s.then(dve.tensor_tensor(v_m[:, t], v_m[:, t], bias[:, t, :].unsqueeze(2).to_broadcast(one), ALU.mult))
            s.then(dve.tensor_tensor(bias[:, :, :], bias[:, :, :], masked_keys[:, :].unsqueeze(2).to_broadcast([P, NT, H0]), ALU.mult))
            s.then(dve.tensor_tensor(row_sum[:, :, :], row_sum[:, :, :], bias[:, :, :], ALU.add))
            s.then(dve.reciprocal(row_sum[:, :, :], row_sum[:, :, :]))
            dve.wait_ge(out_copied, NT * (H0 // G0))
            s.then(dve.tensor_tensor(out[:, :, :, :], out[:, :, :, :], v_m, ALU.add))
            for t in range(NT):
                dve.tensor_tensor(out[:, t], out[:, t], row_sum[:, t, :].unsqueeze(2).to_broadcast(one), ALU.mult).then_inc(out_ready, 1)
            for t in range(NT):
                dve.wait_ge(wo_done, t + 1)
                dve.tensor_tensor(core.x[:, t, :], core.x[:, t, :], aux[:, t % 4, 0:D], ALU.add).then_inc(added, 1)

        @block.tensor
        def _(pe):
            norm.tensor(pe)
            pe.wait_ge(norm.xnT_ready, NT // 2)
            pe.wait_ge(wv_in, 16)
            for t in range(NT):
                for k in range(DC):
                    last = pe.matmul(aux[:, t // 2, t % 2 * D:(t % 2 + 1) * D], core.xnT[:, k, t * P:(t + 1) * P],
                                     wv[:, k, :], start=(k == 0), stop=(k == DC - 1))
                if t % 2:
                    last.then_inc(v_done, 1)
            pe.wait_ge(made, 9)
            pe.wait_ge(later_ready, NT)
            for t in range(NT):
                pe.matmul(acc[:, t // 2, t % 2 * D:(t % 2 + 1) * D], after[:, :], v[:, t, :], start=True, stop=False)
                last = pe.matmul(acc[:, t // 2, t % 2 * D:(t % 2 + 1) * D], ones[:, :], v_later[:, t, :], start=False, stop=True)
                if t % 2:
                    last.then_inc(v_masked_done, 1)
            pe.wait_ge(v_masked_ready, 4)

            def group(g, s):
                for w in range(2):
                    for h in range(2):
                        for k in range(DC):
                            last = pe.matmul(acc[:, 2 * w + h, :], wqk[:, s, k, w * P:(w + 1) * P],
                                             core.xnT[:, k, h * HALF:(h + 1) * HALF],
                                             start=(k == 0), stop=(k == DC - 1))
                    last.then_inc(projected, 1)

                def score(j):
                    n = STEPS0 * g + j
                    t = tile_of(j)
                    w = (t + 1) * P
                    row = PAD0 * (j % G0)
                    if j < 2:
                        pe.wait_ge(qk_ready, 2 * g + 2)
                    else:
                        pe.wait_ge(exp_done, n - 1)
                    for c in range(t // 4 + 1):
                        a, b = c * HALF, min(w, (c + 1) * HALF)
                        last = pe.matmul(acc[:, 2 * (j % 2) + c, 0:b - a], qk[row:row + PAD0, 0, t * P:(t + 1) * P],
                                         qk[row:row + PAD0, 1, a:b], start=True, stop=b < w)
                    pe.matmul(acc[:, 2 * (j % 2) + c, b - a - P:b - a], ident_b[:, :], below[:, :],
                              start=False, stop=True).then_inc(scored, 1)

                def turn(j):
                    n = STEPS0 * g + j
                    before, count = chunks(j)
                    t = tile_of(j)
                    pe.wait_ge(exp_done, n + 1)
                    for c in range(count):
                        k = CHUNKS * g + before + c
                        if before + c >= 2:
                            pe.wait_ge(chunk_copied, k - 1)
                        for b in range(4 * c, min(t + 1, 4 * c + 4)):
                            last = pe.transpose(aux[:, (before + c) % 2, b % 4 * P:(b % 4 + 1) * P],
                                                probs[:, j % 4, b * P:(b + 1) * P], core.ident[:, :])
                        last.then_inc(chunk_turned, 1)

                def weigh(j):
                    before, count = chunks(j)
                    t = tile_of(j)
                    h = j % G0
                    if h == 0 and j >= 2 * G0:
                        pe.wait_ge(out_copied, NT * g + j // G0 - 1)
                    pe.wait_ge(chunk_copied, CHUNKS * g + before + count)
                    for b in range(t + 1):
                        last = pe.matmul(aux[:, 2 + j // G0 % 2, h * HD0:(h + 1) * HD0], probsT[:, j % 4, b * P:(b + 1) * P],
                                         v[:, b, bass.ds(HD0 * (G0 * g + h), HD0)], start=(b == 0), stop=(b == t))
                    if h == G0 - 1:
                        last.then_inc(pv_done, 1)

                steady([(0, score), (2, turn), (4, weigh)])

            with pe.Fori(0, H0 // G0 // 2) as i:
                for s in range(2):
                    pe.wait_ge(wqk_in[s], 32 * i + 32)
                    group(2 * i + s, s)
            pe.wait_ge(wo_in, 16)
            for q in range(NT // 2):
                pe.wait_ge(out_ready, 2 * q + 2)
                for t in (2 * q, 2 * q + 1):
                    for k in range(DC):
                        last = pe.transpose(acc[:, q, (2 * k + t % 2) * P:(2 * k + t % 2 + 1) * P],
                                            out[:, t, k * 8:(k + 1) * 8, :].rearrange("p h d -> p (h d)"), core.ident[:, :])
                last.then_inc(out_turned, 1)
            for t in range(NT):
                pe.wait_ge(outT_ready, t // 2 + 1)
                if t >= 4:
                    pe.wait_ge(added, t - 3)
                for k in range(DC):
                    last = pe.matmul(aux[:, t % 4, 0:D], outT[:, k, t * P:(t + 1) * P], wo[:, k, :],
                                     start=(k == 0), stop=(k == DC - 1))
                last.then_inc(wo_done, 1)



INNER, TAPS = 512, 4
NC = INNER // P


def conv_layer(nc, core, in_dram, out_dram, channel_dram):
    with ExitStack() as ctx:
        def sb(name, shape, dt=F32):
            return ctx.enter_context(nc.sbuf_tensor(f"conv_{name}", shape, dt))

        sem = ctx.enter_context(Sems(nc, "conv"))
        norm = Norm(nc, core, ctx, sem, "conv")
        w_in = sb("w_in", [P, NC, DC, 2 * P])
        w_out = sb("w_out", [P, NC, D])
        channel = sb("channel", [P, NC, TAPS + 2])
        xi = sb("xi", [P, 2, TAPS - 1 + T])
        conv = sb("conv", [P, 2, T])
        gate = sb("gate", [P, 2, T])
        hidden = sb("hidden", [P, 2, T])

        w_in_in = sem("w_in_in")
        w_out_in = sem("w_out_in")
        channel_in = sem("channel_in")
        padded = sem("padded")
        xi_done = sem("xi_done")
        xi_ready = sem("xi_ready")
        gate_done = sem("gate_done")
        gate_ready = sem("gate_ready")
        tap = sem("tap")
        conv_ready = sem("conv_ready")
        silu_ready = sem("silu_ready")
        hidden_ready = sem("hidden_ready")
        out_done = sem("out_done")
        added = sem("added")
        acc, aux = core.acc, core.aux
        block = ctx.enter_context(nc.Block())

        @block.sync
        def _(sp):
            sp.dma_start(channel[:, :, :], channel_dram).then_inc(channel_in, 16)
            sp.dma_start(w_in[:, :, :, :], in_dram.rearrange("f p k n -> p f k n")).then_inc(w_in_in, 16)
            sp.dma_start(w_out[:, :, :], out_dram.rearrange("f p n -> p f n")).then_inc(w_out_in, 16)

        @block.gpsimd
        def _(pool):
            pool.memset(xi[:, :, 0:TAPS - 1], 0.0).then_inc(padded, 1)
            norm.gpsimd(pool)

        @block.scalar
        def _(act):
            norm.scalar(act)
            for f in range(NC + 1):
                if f < NC:
                    act.wait_ge(xi_done, f + 1)
                    if f >= 2:
                        act.wait_ge(conv_ready, f - 1)
                    act.activation(xi[:, f % 2, TAPS - 1:], aux[:, 0:2, :].rearrange("p a b -> p (a b)"),
                                   ACT.Copy).then_inc(xi_ready, 1)
                    act.wait_ge(gate_done, f + 1)
                    act.activation(gate[:, f % 2], aux[:, 2:4, :].rearrange("p a b -> p (a b)"),
                                   ACT.Silu).then_inc(gate_ready, 1)
                if f >= 1:
                    r = f - 1
                    act.wait_ge(conv_ready, r + 1)
                    act.activation(conv[:, r % 2], conv[:, r % 2], ACT.Silu,
                                   bias=channel[:, r, TAPS:TAPS + 1]).then_inc(silu_ready, 1)

        @block.vector
        def _(dve):
            norm.vector(dve)
            dve.wait_ge(padded, 1)
            dve.wait_ge(channel_in, 16)
            for f in range(NC + 1):
                if f < NC:
                    dve.wait_ge(xi_ready, f + 1)
                    if f >= 2:
                        dve.wait_ge(hidden_ready, f - 1)
                    dve.tensor_scalar(conv[:, f % 2], xi[:, f % 2, 0:T], channel[:, f, 0:1], None, ALU.mult).then_inc(tap, 1)
                    for k in range(1, TAPS):
                        dve.wait_ge(tap, (TAPS - 1) * f + k)
                        dve.scalar_tensor_tensor(conv[:, f % 2], xi[:, f % 2, k:k + T], channel[:, f, k:k + 1],
                                                 conv[:, f % 2], ALU.mult, ALU.add).then_inc(tap if k < TAPS - 1 else conv_ready, 1)
                if f >= 1:
                    r = f - 1
                    dve.wait_ge(silu_ready, r + 1)
                    dve.wait_ge(gate_ready, r + 1)
                    if r >= 2:
                        dve.wait_ge(out_done, r - 1)
                    dve.scalar_tensor_tensor(hidden[:, r % 2], conv[:, r % 2], channel[:, r, TAPS + 1:TAPS + 2],
                                             gate[:, r % 2], ALU.mult, ALU.mult).then_inc(hidden_ready, 1)
            dve.wait_ge(out_done, NC)
            for q in range(4):
                dve.tensor_tensor(core.x[:, 2 * q:2 * q + 2, :], core.x[:, 2 * q:2 * q + 2, :],
                                  acc[:, q, :].rearrange("p (t d) -> p t d", t=2), ALU.add).then_inc(added, 1)

        @block.tensor
        def _(pe):
            norm.tensor(pe)
            pe.wait_ge(norm.xnT_ready, NT // 2)
            for q in range(4):
                pe.matmul(acc[:, q, :], core.zeros[:, 0:P], core.zeros[:, :], start=True, stop=True, skip_group_check=True)
            pe.wait_ge(w_in_in, 16)
            pe.wait_ge(w_out_in, 16)
            for f in range(NC + 1):
                if f < NC:
                    for w, done, read in ((0, xi_done, xi_ready), (1, gate_done, gate_ready)):
                        if f >= 1:
                            pe.wait_ge(read, f)
                        for h in range(2):
                            for k in range(DC):
                                last = pe.matmul(aux[:, 2 * w + h, :], w_in[:, f, k, w * P:(w + 1) * P],
                                                 core.xnT[:, k, h * HALF:(h + 1) * HALF],
                                                 start=(k == 0), stop=(k == DC - 1))
                        last.then_inc(done, 1)
                if f >= 1:
                    r = f - 1
                    pe.wait_ge(hidden_ready, r + 1)
                    for t in range(NT):
                        last = pe.matmul(acc[:, t // 2, t % 2 * D:(t % 2 + 1) * D], hidden[:, r % 2, t * P:(t + 1) * P],
                                         w_out[:, r, :], start=False, stop=False, skip_group_check=True)
                    last.then_inc(out_done, 1)


STATE, RANK = 16, 128


def scan_layer(nc, core, in_dram, bc_dram, dt_dram, channel_dram, a_log_dram):
    with ExitStack() as ctx:
        def sb(name, shape, dt=F32):
            return ctx.enter_context(nc.sbuf_tensor(f"scan_{name}", shape, dt))

        sem = ctx.enter_context(Sems(nc, "scan"))
        norm = Norm(nc, core, ctx, sem, "scan")
        ROWS = 2 * STATE
        w_delta = sb("w_delta", [P, DC, RANK])
        w_bc = sb("w_bc", [P, DC, ROWS])
        w_dt = sb("w_dt", [P, DC, P])
        channel = sb("channel", [P, DC, 2])
        a = sb("a", [P, DC, STATE])
        pick = sb("pick", [P, ROWS, P], BF16)
        low = sb("low", [P, T])
        parts = sb("parts", [P, T], BF16)
        rest = sb("rest", [ROWS, 2, T])
        part32 = sb("part32", [ROWS, 2, T])
        z = sb("z", [P, DC, T])
        delta = sb("delta", [P, DC, T])
        du = sb("du", [P, DC, T])
        b_all = sb("b_all", [P, 2, T])
        decay = sb("decay", [P, 4, T])
        dbu = sb("dbu", [P, 4, T])
        h = sb("h", [P, 4, T])
        hc = sb("hc", [P, 4, T])

        w_in = sem("w_in")
        channel_in = sem("channel_in")
        made = sem("made")
        a_ready = sem("a_ready")
        low_done = sem("low_done")
        low_ready = sem("low_ready")
        bc_done = sem("bc_done")
        split = sem("split")
        parts_ready = sem("parts_ready")
        dt_done = sem("dt_done")
        abs_ready = sem("abs_ready")
        soft = sem("soft")
        log_ready = sem("log_ready")
        relu_ready = sem("relu_ready")
        delta_ready = sem("delta_ready")
        du_ready = sem("du_ready")
        b_spread = sem("b_spread")
        c_spread = sem("c_spread")
        b_ready = sem("b_ready")
        decay_ready = sem("decay_ready")
        dbu_ready = sem("dbu_ready")
        h_ready = sem("h_ready")
        hc_ready = sem("hc_ready")
        summed = sem("summed")
        y_ready = sem("y_ready")
        y_turned = sem("y_turned")
        added = sem("added")
        acc, aux = core.acc, core.aux
        block = ctx.enter_context(nc.Block())

        @block.sync
        def _(sp):
            for dst, src in ((w_delta, in_dram), (w_bc, bc_dram), (w_dt, dt_dram)):
                sp.dma_start(dst[:, :, :], src).then_inc(w_in, 16)
            for dst, src in ((channel, channel_dram), (a, a_log_dram)):
                sp.dma_start(dst[:, :, :], src).then_inc(channel_in, 16)

        @block.gpsimd
        def _(pool):
            norm.gpsimd(pool)
            pool.wait_ge(norm.rstd_ready, 1)
            pool.memset(pick[:, :, :], 0.0).then_inc(made, 1)
            pool.wait_ge(made, 1)
            pool.memset(parts[96:128, :], 0.0).then_inc(made, 1)
            for q in range(3):
                pool.wait_ge(made, q + 2)
                pool.affine_select(out=pick[32 * q:32 * q + 32, :, :], in_=pick[32 * q:32 * q + 32, :, :],
                                   compare_op=ALU.not_equal, fill=1.0, base=0,
                                   pattern=[[-1, ROWS], [0, P]], channel_multiplier=1).then_inc(made, 1)
            pool.wait_ge(made, 5)
            for k in range(DC):
                pool.wait_ge(delta_ready, k + 1)
                pool.tensor_tensor(du[:, k], delta[:, k], core.xnT[:, k], ALU.mult).then_inc(du_ready, 1)
            pool.wait_ge(du_ready, DC)
            with pool.Fori(0, STATE // 2) as i:
                for s in range(2):
                    for k in range(DC):
                        m = 4 * i + 2 * s + k
                        if k == 0:
                            pool.wait_ge(b_ready, 2 * i + s + 1)
                        pool.tensor_tensor(dbu[:, 2 * s + k], du[:, k], b_all[:, s], ALU.mult).then_inc(dbu_ready, 1)

        @block.scalar
        def _(act):
            norm.scalar(act)
            act.wait_ge(low_done, 1)
            act.activation(low[:, :], acc[:, 0:2, :].rearrange("p a b -> p (a b)"), ACT.Copy).then_inc(low_ready, 1)
            act.wait_ge(channel_in, 32)
            act.activation(a[:, :, :], a[:, :, :], ACT.Exp).then_inc(a_ready, 1)
            for k in range(DC):
                act.wait_ge(dt_done, k + 1)
                act.activation(z[:, k], acc[:, 2 * k:2 * k + 2, :].rearrange("p a b -> p (a b)"), ACT.Abs,
                               bias=channel[:, k, 0:1]).then_inc(abs_ready, 1)
            for k in range(DC):
                act.wait_ge(abs_ready, k + 1)
                act.activation(z[:, k], z[:, k], ACT.Exp, scale=-1.0).then_inc(soft, 1)
            for k in range(DC):
                act.wait_ge(soft, k + 1)
                act.activation(z[:, k], z[:, k], ACT.Ln, bias=1.0).then_inc(log_ready, 1)
            act.wait_ge(delta_ready, DC)
            act.wait_ge(a_ready, 2)

            with act.Fori(0, STATE // 2) as i:
                for s in range(2):
                    n = 2 * i + s
                    act.wait_ge(b_spread, n + 1)
                    act.activation(b_all[:, s], aux[:, 0:2, :].rearrange("p a b -> p (a b)"), ACT.Copy).then_inc(b_ready, 1)
                    for k in range(DC):
                        act.activation(decay[:, 2 * s + k], delta[:, k], ACT.Exp,
                                       scale=a[:, k, bass.ds(n, 1)]).then_inc(decay_ready, 1)

        @block.vector
        def _(dve):
            norm.vector(dve)
            dve.wait_ge(a_ready, 1)
            dve.tensor_scalar(a[:, :, :], a[:, :, :], -1.0, None, ALU.mult).then_inc(a_ready, 1)
            dve.wait_ge(bc_done, 1)
            bc = aux[0:ROWS, 0:2, :].rearrange("p a b -> p (a b)")
            s = Steps(dve, split)
            s.then(dve.tensor_copy(parts[0:32, :], bc))
            s.then(dve.tensor_copy(part32[:, 0], parts[0:32, :]))
            s.then(dve.tensor_tensor(rest[:, 0], bc, part32[:, 0], ALU.subtract))
            s.then(dve.tensor_copy(parts[32:64, :], rest[:, 0]))
            s.then(dve.tensor_copy(part32[:, 1], parts[32:64, :]))
            s.then(dve.tensor_tensor(rest[:, 1], rest[:, 0], part32[:, 1], ALU.subtract))
            dve.tensor_copy(parts[64:96, :], rest[:, 1]).then_inc(parts_ready, 1)
            for k in range(DC):
                dve.wait_ge(abs_ready, k + 1)
                dve.tensor_scalar(delta[:, k], acc[:, 2 * k:2 * k + 2, :].rearrange("p a b -> p (a b)"),
                                  channel[:, k, 0:1], 0.0, ALU.add, ALU.max).then_inc(relu_ready, 1)
            for k in range(DC):
                dve.wait_ge(log_ready, k + 1)
                dve.wait_ge(relu_ready, k + 1)
                dve.tensor_tensor(delta[:, k], delta[:, k], z[:, k], ALU.add).then_inc(delta_ready, 1)

            with dve.Fori(0, STATE // 2) as i:
                for s2 in range(2):
                    n = 2 * i + s2
                    for k in range(DC):
                        m = 2 * n + k
                        dve.wait_ge(decay_ready, m + 1)
                        dve.wait_ge(dbu_ready, m + 1)
                        dve.tensor_tensor_scan(h[:, 2 * s2 + k], decay[:, 2 * s2 + k], dbu[:, 2 * s2 + k], 0.0,
                                               ALU.mult, ALU.add).then_inc(h_ready, 1)
                    dve.wait_ge(c_spread, n + 1)
                    for k in range(DC):
                        dve.wait_ge(h_ready, 2 * n + k + 1)
                        dve.tensor_tensor(hc[:, 2 * s2 + k], h[:, 2 * s2 + k], aux[:, 2:4, :].rearrange("p a b -> p (a b)"),
                                          ALU.mult).then_inc(hc_ready, 1)
            dve.wait_ge(summed, STATE * DC)
            for k in range(DC):
                dve.scalar_tensor_tensor(z[:, k], core.xnT[:, k], channel[:, k, 1:2],
                                         acc[:, 2 * k:2 * k + 2, :].rearrange("p a b -> p (a b)"),
                                         ALU.mult, ALU.add).then_inc(y_ready, 1)
            for q in range(4):
                dve.wait_ge(y_turned, q + 1)
                dve.tensor_tensor(core.x[:, 2 * q:2 * q + 2, :], core.x[:, 2 * q:2 * q + 2, :],
                                  aux[:, q, :].rearrange("p (t d) -> p t d", t=2), ALU.add).then_inc(added, 1)

        @block.tensor
        def _(pe):
            norm.tensor(pe)
            pe.wait_ge(norm.xnT_ready, NT // 2)
            pe.wait_ge(w_in, 48)

            def project(out, w, rhs, chunks):
                for hf in range(2):
                    for k in range(chunks):
                        last = pe.matmul(out[:, hf, :], w(k), rhs(k)[:, hf * HALF:(hf + 1) * HALF],
                                         start=(k == 0), stop=(k == chunks - 1))
                return last

            project(acc[:, 0:2, :], lambda k: w_delta[:, k, :], lambda k: core.xnT[:, k], DC).then_inc(low_done, 1)
            project(aux[0:ROWS, 0:2, :], lambda k: w_bc[:, k, :], lambda k: core.xnT[:, k], DC).then_inc(bc_done, 1)
            pe.wait_ge(low_ready, 1)
            for k in range(DC):
                project(acc[:, 2 * k:2 * k + 2, :], lambda _: w_dt[:, k, :], lambda _: low, 1).then_inc(dt_done, 1)
            pe.wait_ge(parts_ready, 1)
            pe.wait_ge(made, 5)
            pe.wait_ge(relu_ready, DC)
            for q in range(4):
                pe.matmul(acc[:, q, :], core.zeros[:, 0:P], core.zeros[:, :], start=True, stop=True, skip_group_check=True)

            def spread(bank, row, done):
                for hf in range(2):
                    last = pe.matmul(aux[:, bank + hf, :], pick[:, bass.ds(row, 1), :].rearrange("p a m -> p (a m)"),
                                     parts[:, hf * HALF:(hf + 1) * HALF], start=True, stop=True)
                last.then_inc(done, 1)

            def sums(i, s):
                for k in range(DC):
                    pe.wait_ge(hc_ready, 4 * i + 2 * s + k + 1)
                    for hf in range(2):
                        last = pe.matmul(acc[:, 2 * k + hf, :], core.ident[:, :], hc[:, 2 * s + k, hf * HALF:(hf + 1) * HALF],
                                         start=False, stop=False, skip_group_check=True)
                    last.then_inc(summed, 1)

            spread(0, 0, b_spread)
            spread(2, STATE, c_spread)

            def state(i, s):
                pe.wait_ge(b_ready, 2 * i + s + 1)
                spread(0, 2 * i + s + 1, b_spread)
                sums(i, s)
                spread(2, STATE + 2 * i + s + 1, c_spread)

            with pe.Fori(0, STATE // 2 - 1) as i:
                for s in range(2):
                    state(i, s)
            state(STATE // 2 - 1, 0)
            sums(STATE // 2 - 1, 1)
            for q in range(NT // 2):
                pe.wait_ge(y_ready, DC)
                for t in (2 * q, 2 * q + 1):
                    for k in range(DC):
                        last = pe.transpose(aux[:, q, (t % 2) * D + k * P:(t % 2) * D + (k + 1) * P],
                                            z[:, k, t * P:(t + 1) * P], core.ident[:, :])
                last.then_inc(y_turned, 1)


def store(nc, core, out_dram):
    with ExitStack() as ctx:
        stored = ctx.enter_context(nc.semaphore("stored"))
        block = ctx.enter_context(nc.Block())

        @block.sync
        def _(sp):
            sp.dma_start(out_dram.rearrange("(n p) d -> p n d", p=P), core.x[:, :, :]).then_inc(stored, 16)
            sp.wait_ge(stored, 16)


def build(nc, a, out_dram):
    comb_dram = nc.dram_tensor("comb_by_expert", (E, T), F32, kind="Internal").ap()
    with ExitStack() as ctx:
        core = Core(nc, ctx)
        constants(nc, core, a["x"])
        masked_attention_layer(nc, core, a["a0_wq"], a["a0_wk"], a["a0_wv"], a["a0_wo"])
        ffn_layer(nc, core, "f1", a["f0_up"], a["f0_down"], a["f0_router"], a["f0_bias"], comb_dram, 8)
        conv_layer(nc, core, a["c_in"], a["c_out"], a["c_channel"])
        ffn_layer(nc, core, "f2", a["f0_up"], a["f0_down"], a["f0_router"], a["f0_bias"], comb_dram, 8)
        scan_layer(nc, core, a["s_in"], a["s_bc"], a["s_dt"], a["s_channel"], a["s_a_log"])
        ffn_layer(nc, core, "f3", a["f1_up"], a["f1_down"], a["f1_router"], None, comb_dram, 0)
        gqa_layer(nc, core, a["g_wq"], a["g_wk"], a["g_wv"], a["g_wo"], a["g_norm_w"], a["cos"], a["sin"])
        ffn_layer(nc, core, "f4", a["f1_up"], a["f1_down"], a["f1_router"], None, comb_dram, 0)
        store(nc, core, out_dram)


def layouts(inputs):
    import numpy as np

    i = {k: np.asarray(v) for k, v in inputs.items()}

    def rows(w):
        return w.reshape(-1, P, w.shape[-1]).transpose(1, 0, 2)

    def blocks(w, n):
        return w.reshape(DC, P, n, -1).transpose(2, 1, 0, 3)

    def heads(w):
        padded = np.zeros((D, H0 // G0, G0, PAD0), w.dtype)
        padded[..., :HD0] = w.reshape(D, H0 // G0, G0, HD0)
        return blocks(padded.reshape(D, -1), H0 // G0)

    a = {"x": i["L0_attn_a_x"].reshape(T, D)}
    a["a0_wq"], a["a0_wk"] = heads(i["L0_attn_a_Wq"]), heads(i["L0_attn_a_Wk"])
    a["a0_wv"], a["a0_wo"] = rows(i["L0_attn_a_Wv"]), rows(i["L0_attn_a_Wo"])
    w12 = i["L0_ffn_w12"]
    gates = np.concatenate([w12[:, :P], i["L0_ffn_sw1"].reshape(8, P, D)])
    ups = np.concatenate([w12[:, P:], i["L0_ffn_sw2"].reshape(8, P, D)])
    both = np.concatenate([gates, ups], 1).transpose(0, 2, 1)
    a["f0_up"] = both.reshape(E, DC, P, 2 * P).transpose(0, 2, 1, 3)
    a["f0_down"] = np.concatenate([i["L0_ffn_w3"].transpose(0, 2, 1), i["L0_ffn_sw3"].T.reshape(8, P, D)])
    a["f0_router"] = rows(i["L0_ffn_router_w"].T)
    a["f0_bias"] = i["L0_ffn_expert_bias"]
    w_in = i["L0_attn_b_w_in"].reshape(2, NC, P, DC, P)
    a["c_in"] = w_in.transpose(1, 4, 3, 0, 2).reshape(NC, P, DC, 2 * P)
    a["c_out"] = i["L0_attn_b_w_out"].T.reshape(NC, P, D)
    channel = np.concatenate([i["L0_attn_b_conv_w"][:, 0], i["L0_attn_b_conv_b"][:, None], i["L0_attn_b_D"][:, None]], 1)
    a["c_channel"] = rows(channel)
    x_proj = i["L1_attn_a_x_proj_w"].T
    a["s_in"], a["s_bc"] = rows(x_proj[:, :RANK]), rows(x_proj[:, RANK:])
    a["s_dt"] = i["L1_attn_a_dt_proj_w"].T.reshape(RANK, DC, P)
    a["s_channel"] = rows(np.stack([i["L1_attn_a_dt_proj_b"], i["L1_attn_a_D"]], 1))
    a["s_a_log"] = rows(i["L1_attn_a_A_log"])
    both = np.concatenate([i["L1_ffn_wg"], i["L1_ffn_wu"]], 2)
    a["f1_up"] = both.reshape(E, DC, P, 2 * P).transpose(0, 2, 1, 3)
    a["f1_down"] = i["L1_ffn_wd"]
    a["f1_router"] = rows(i["L1_ffn_gate_w"].T)
    for name in ("q", "k", "v"):
        a[f"g_w{name}"] = blocks(i[f"L1_attn_b_W{name}"], KV)
    a["g_wo"] = i["L1_attn_b_Wo"].reshape(KV, GQ, HD, D).transpose(0, 2, 1, 3)
    a["g_norm_w"] = np.stack([i["L1_attn_b_k_norm_w"], i["L1_attn_b_q_norm_w"]], 1)
    inv_freq = (1.0 / np.float32(1000000.0) ** (np.arange(0, HD, 2, dtype=np.float32) / np.float32(HD))).astype(np.float32)
    angle = np.outer(np.concatenate([inv_freq, inv_freq]), np.arange(T, dtype=np.float32)).astype(np.float32)
    a["cos"], a["sin"] = np.cos(angle), np.sin(angle)
    return {k: np.ascontiguousarray(v) for k, v in a.items()}


def kernel(**inputs):
    import numpy as np
    import concourse.bacc as bacc
    from concourse.bass_utils import run_bass_kernel_spmd

    nc = bacc.Bacc("TRN2", target_bir_lowering=False, num_devices=1)
    arrays, aps = {}, {}
    for name, array in layouts(inputs).items():
        arrays[f"in_{name}"] = array
        aps[name] = nc.dram_tensor(f"in_{name}", array.shape, mybir.dt.from_np(array.dtype), kind="ExternalInput").ap()
    out = nc.dram_tensor("out_stream", (T, D), F32, kind="ExternalOutput").ap()
    build(nc, aps, out)
    result = run_bass_kernel_spmd(nc, [arrays], core_ids=[0])
    return np.asarray(result.results[0]["out_stream"]).reshape(1, T, D)
```

```python
from contextlib import ExitStack

import concourse.bass as bass
from concourse import mybir

F32 = mybir.dt.float32
F32R = mybir.dt.float32r
BF16 = mybir.dt.bfloat16
ALU = mybir.AluOpType
ACT = mybir.ActivationFunctionType
AX = mybir.AxisListType.X

P = 128
T, D = 1024, 256
NT = T // P
DC = D // P
HALF = 512
LN_EPS = 1e-5
E = 16
BIG = 1e30


class Steps:

    def __init__(self, eng, sem):
        self.eng, self.sem, self.n = eng, sem, 0

    def then(self, ins):
        self.n += 1
        ins.then_inc(self.sem, 1)
        self.eng.wait_ge(self.sem, self.n)


class Sems:

    def __init__(self, nc, tag):
        self.nc, self.tag, self.all = nc, tag, []

    def __enter__(self):
        return self

    def __call__(self, name):
        self.all.append(self.nc.alloc_semaphore(f"{self.tag}_{name}"))
        return self.all[-1]

    def __exit__(self, *_):
        self.nc.clear_and_free_semaphores(self.all)
        self.nc.all_engine_barrier()


class Core:

    def __init__(self, nc, ctx):
        def sb(name, shape, dt=F32):
            return ctx.enter_context(nc.sbuf_tensor(name, shape, dt))

        self.nc = nc
        self.x = sb("stream", [P, NT, D])
        self.xnT = sb("xnT", [P, DC, T])
        self.xnT_high = sb("xnT_high", [P, DC, T], F32R)
        self.xnT_low = sb("xnT_low", [P, DC, T], F32R)
        self.ident = sb("ident", [P, P])
        self.zeros = sb("zeros", [P, HALF], BF16)
        self.minus_half = sb("minus_half", [P, NT])
        self.acc = ctx.enter_context(nc.psum_tensor("acc", [P, 4, HALF], F32))
        self.aux = ctx.enter_context(nc.psum_tensor("aux", [P, 4, HALF], F32))


def start(i):
    return isinstance(i, int) and i == 0


def pipeline(eng, steps, stages, body, done=0, lead=None):
    lead = lead or max(max(lag for lag, _ in stages) + 2, 4)
    for n in range(done, lead):
        for lag, stage in stages:
            if n >= lag:
                stage(0, n - lag)
    rounds = (steps - lead) // body
    with eng.Fori(0, rounds) as i:
        for j in range(lead, lead + body):
            for lag, stage in stages:
                stage(i, j - lag)
    for j in range(lead, steps - body * rounds + lead):
        for lag, stage in stages:
            if j - lag < steps - body * rounds:
                stage(rounds, j - lag)


def three(w_high, w_low, x_high, x_low):
    return ((w_high, x_high), (w_high, x_low), (w_low, x_high))


def constants(nc, core, x_dram):
    with ExitStack() as ctx:
        sem = ctx.enter_context(Sems(nc, "start"))
        x_in = sem("x_in")
        filled = sem("filled")
        block = ctx.enter_context(nc.Block())

        @block.sync
        def _(sp):
            sp.dma_start(core.x[:, :, :], x_dram.rearrange("(n p) d -> p n d", p=P)).then_inc(x_in, 16)
            sp.wait_ge(x_in, 16)

        @block.gpsimd
        def _(pool):
            pool.memset(core.ident[:, :], 0.0).then_inc(filled, 1)
            pool.wait_ge(filled, 1)
            pool.affine_select(out=core.ident[:, :], in_=core.ident[:, :], compare_op=ALU.not_equal,
                               fill=1.0, base=0, pattern=[[-1, P]], channel_multiplier=1)
            pool.memset(core.zeros[:, :], 0.0)
            pool.memset(core.minus_half[:, :], -0.5)


class Norm:

    def __init__(self, nc, core, ctx, sem, tag, whole=True):
        def sb(name, shape, dt=F32):
            return ctx.enter_context(nc.sbuf_tensor(f"{tag}_{name}", shape, dt))

        self.core = core
        self.whole = whole
        self.stats = sb("ln_stats", [P, NT, 6])
        self.mv = sb("ln_mean_var", [P, NT, 2])
        self.rstd = sb("ln_rstd", [P, NT])
        self.xn = sb("ln_xn", [P, NT, D])
        self.stats_done = sem("stats_done")
        self.var_ready = sem("var_ready")
        self.eps_added = sem("eps_added")
        self.rstd_ready = sem("rstd_ready")
        self.xn_ready = sem("xn_ready")
        self.turned = sem("turned")
        self.xnT_ready = sem("xnT_ready")
        self.high_ready = sem("xnT_high_ready")
        self.low_ready = sem("xnT_low_ready")

    def vector(self, dve):
        c = self.core

        def statistics(q):
            for t in (2 * q, 2 * q + 1):
                dve.bn_stats(self.stats[:, t, :], c.x[:, t, :]).then_inc(self.stats_done, 1)
            for t in (2 * q, 2 * q + 1):
                dve.wait_ge(self.stats_done, t + 1)
                dve.bn_aggr(self.mv[:, t, :], self.stats[:, t, :]).then_inc(self.var_ready, 1)

        def scale(q):
            dve.wait_ge(self.rstd_ready, q + 1)
            for t in (2 * q, 2 * q + 1):
                dve.tensor_scalar(self.xn[:, t, :], c.x[:, t, :], self.mv[:, t, 0:1], self.rstd[:, t:t + 1],
                                  ALU.subtract, ALU.mult).then_inc(self.xn_ready, 1)

        def low(q):
            dve.wait_ge(self.high_ready, q + 1)
            pair = slice(2 * q * P, (2 * q + 2) * P)
            dve.tensor_tensor(c.xnT_low[:, :, pair], c.acc[:, q, :].rearrange("p (k t) -> p k t", k=DC),
                              c.xnT_high[:, :, pair].bitcast(F32), ALU.subtract).then_inc(self.low_ready, 1)

        for q in range(NT // 2 + 3):
            if q < NT // 2:
                statistics(q)
            if 1 <= q < NT // 2 + 1:
                scale(q - 1)
            if q >= 3:
                low(q - 3)

    def gpsimd(self, pool):
        for q in range(NT // 2):
            two = slice(2 * q, 2 * q + 2)
            pool.wait_ge(self.var_ready, 2 * q + 2)
            pool.tensor_scalar(self.rstd[:, two], self.mv[:, two, 1], LN_EPS, None, ALU.add).then_inc(self.eps_added, 1)
            pool.wait_ge(self.eps_added, q + 1)
            pool.tensor_tensor(self.rstd[:, two], self.rstd[:, two], self.core.minus_half[:, two],
                               ALU.pow).then_inc(self.rstd_ready, 1)

    def tensor(self, pe):
        c = self.core
        for q in range(NT // 2):
            pe.wait_ge(self.xn_ready, 2 * q + 2)
            for t in (2 * q, 2 * q + 1):
                for k in range(DC):
                    last = pe.transpose(c.acc[:, q, (2 * k + t % 2) * P:(2 * k + t % 2 + 1) * P],
                                        self.xn[:, t, k * P:(k + 1) * P], c.ident[:, :])
            last.then_inc(self.turned, 1)

    def scalar(self, act):
        c = self.core
        for q in range(NT // 2):
            act.wait_ge(self.turned, q + 1)
            act.activation(c.xnT_high[:, :, 2 * q * P:(2 * q + 2) * P],
                           c.acc[:, q, :].rearrange("p (k t) -> p k t", k=DC), ACT.Copy).then_inc(self.high_ready, 1)
        for q in range(NT // 2 if self.whole else 0):
            act.wait_ge(self.low_ready, q + 1)
            act.activation(c.xnT[:, :, 2 * q * P:(2 * q + 2) * P],
                           c.acc[:, q, :].rearrange("p (k t) -> p k t", k=DC),
                           ACT.Copy).then_inc(self.xnT_ready, 1)


def ffn_layer(nc, core, tag, up_dram, down_dram, router_dram, bias_dram, comb_dram, shared):
    routed = E - shared
    UP = DC * 2 * P
    SLOTS = 4
    with ExitStack() as ctx:
        def sb(name, shape, dt=F32):
            return ctx.enter_context(nc.sbuf_tensor(f"{tag}_{name}", shape, dt))

        sem = ctx.enter_context(Sems(nc, tag))
        norm = Norm(nc, core, ctx, sem, tag)
        w = sb("w", [P, 2, UP + D])
        w_high = sb("w_high", [P, SLOTS, UP + D], F32R)
        w_low = sb("w_low", [P, SLOTS, UP + D], F32R)
        silu_g = sb("silu_g", [P, 2, HALF])
        hidden = sb("hidden", [P, SLOTS, HALF])
        weighted = sb("weighted", [P, SLOTS, HALF])
        high = sb("high", [P, SLOTS, HALF], F32R)
        low = sb("low", [P, SLOTS, HALF], F32R)
        comb_all = sb("comb_all", [P, 2, T])
        w_router = sb("w_router", [P, DC, routed])
        bias = sb("bias", [P, routed])
        probs = sb("probs", [P, NT, routed])
        select = sb("select", [P, NT, routed])
        rank = sb("rank", [P, NT, routed])
        falling = sb("falling", [P, NT, routed])
        first = sb("first", [P, NT, routed])
        second = sb("second", [P, NT, routed])
        comb = sb("comb", [P, NT, routed])
        stat = sb("stat", [P, NT])
        combT = sb("combT", [routed, T])

        router_in = sem("router_in")
        iota_done = sem("iota_done")
        logits_ready = sem("logits_ready")
        shifted = sem("shifted")
        exp_ready = sem("exp_ready")
        comb_ready = sem("comb_ready")
        combT_turned = sem("combT_turned")
        combT_ready = sem("combT_ready")
        comb_stored = sem("comb_stored")
        comb_in = [sem("comb_in0"), sem("comb_in1")]
        w_in = [sem("w_in0"), sem("w_in1")]
        w_high_ready = sem("w_high_ready")
        w_low_ready = sem("w_low_ready")
        g_ready = sem("g_ready")
        u_ready = sem("u_ready")
        silu_ready = sem("silu_ready")
        hidden_ready = sem("hidden_ready")
        weighted_ready = sem("weighted_ready")
        high_ready = sem("high_ready")
        low_ready = sem("low_ready")
        down_done = sem("down_done")
        small = sem("small")
        added = sem("added")
        acc, aux = core.acc, core.aux
        block = ctx.enter_context(nc.Block())

        @block.sync
        def _(sp):
            sp.dma_start(w_router[:, :, :], router_dram).then_inc(router_in, 16)
            if bias_dram is not None:
                sp.dma_start(bias[:, :], bias_dram.rearrange("(a e) -> a e", a=1).to_broadcast([P, routed])).then_inc(router_in, 16)

            def load(e, s):
                sp.dma_start(w[:, s, 0:UP], up_dram[bass.ds(e, 1)].rearrange("a p k n -> (a p) (k n)")).then_inc(w_in[s], 16)
                sp.dma_start(w[:, s, UP:], down_dram[bass.ds(e, 1)].rearrange("a p n -> (a p) n")).then_inc(w_in[s], 16)

            def load_next(i, s):
                sp.wait_ge(w_low_ready, 2 * i + s - 1)
                load(2 * i + s, s)

            def load_comb(e, s):
                sp.dma_start(comb_all[:, s, :], comb_dram[bass.ds(e - shared, 1), :].to_broadcast([P, T])).then_inc(comb_in[s], 16)

            for s in range(2):
                load(s, s)
            if shared:
                with sp.Fori(1, shared // 2) as i:
                    for s in range(2):
                        load_next(i, s)
            sp.wait_ge(combT_ready, 2)
            sp.dma_start(comb_dram[0:routed, :], combT[:, :]).then_inc(comb_stored, 16)
            sp.wait_ge(comb_stored, 16)
            if not shared:
                for s in range(2):
                    load_comb(s, s)
            with sp.Fori(shared // 2 if shared else 1, E // 2) as i:
                for s in range(2):
                    load_next(i, s)
                    sp.wait_ge(weighted_ready, 4 * i + 2 * s - 2)
                    load_comb(2 * i + s, s)

        @block.gpsimd
        def _(pool):
            for t in range(NT):
                pool.iota(falling[:, t, :], [[-1, routed]], base=routed, channel_multiplier=0,
                          allow_small_or_imprecise_dtypes=True).then_inc(iota_done, 1)
            norm.gpsimd(pool)
            if shared:
                for s in range(2):
                    pool.memset(comb_all[:, s, :], 1.0).then_inc(comb_in[s], 16 * shared // 2)

            def weigh(i, j):
                pool.wait_ge(comb_in[j // 2 % 2], 32 * i + 16 * (j // 4) + 16)
                pool.wait_ge(hidden_ready, 8 * i + j + 1)
                if not (start(i) and j < SLOTS):
                    pool.wait_ge(low_ready, 8 * i + j - SLOTS + 1)
                pool.tensor_tensor(weighted[:, j % SLOTS], hidden[:, j % SLOTS],
                                   comb_all[:, j // 2 % 2, j % 2 * HALF:(j % 2 + 1) * HALF], ALU.mult).then_inc(weighted_ready, 1)

            pipeline(pool, 2 * E, [(0, weigh)], 8)

        @block.scalar
        def _(act):
            def split(i, j):
                if j % 2 == 0:
                    e = 4 * i + j // 2
                    act.wait_ge(w_in[j // 2 % 2], 64 * i + 32 * (j // 4) + 32)
                    if not (start(i) and j < 2 * SLOTS):
                        act.wait_ge(down_done, 2 * (e - SLOTS) + 2)
                    act.activation(w_high[:, j // 2 % SLOTS, :], w[:, j // 2 % 2, :], ACT.Copy).then_inc(w_high_ready, 1)

            def silu(i, j):
                n = 8 * i + j
                act.wait_ge(g_ready, n + 1)
                if not (start(i) and j < 2):
                    act.wait_ge(hidden_ready, n - 1)
                act.activation(silu_g[:, j % 2], aux[:, j % 2 * 2, :], ACT.Silu).then_inc(silu_ready, 1)

            split(0, 0)
            split(0, 2)
            norm.scalar(act)
            silu(0, 0)
            act.wait_ge(logits_ready, 1)
            if shared:
                act.activation(select[:, :, :], acc[:, 0, 0:NT * routed].rearrange("p (t e) -> p t e", e=routed),
                               ACT.Exp, scale=-1.0).then_inc(exp_ready, 1)
            else:
                act.wait_ge(shifted, 1)
                act.activation(probs[:, :, :], select[:, :, :], ACT.Exp).then_inc(exp_ready, 1)
            for h in range(2):
                act.wait_ge(combT_turned, 4 * h + 4)
                act.activation(combT[:, h * HALF:(h + 1) * HALF], acc[0:routed, 1 + h, :], ACT.Copy).then_inc(combT_ready, 1)

            def round_high(i, j):
                n = 8 * i + j
                act.wait_ge(weighted_ready, n + 1)
                if not (start(i) and j < SLOTS):
                    act.wait_ge(down_done, n - SLOTS + 1)
                act.activation(high[:, j % SLOTS], weighted[:, j % SLOTS], ACT.Copy).then_inc(high_ready, 1)

            pipeline(act, 2 * E, [(3, silu), (0, split), (4, round_high)], 8, 4, 2 * SLOTS)

        @block.vector
        def _(dve):
            def split(i, j):
                if j % 2 == 0:
                    dve.wait_ge(w_high_ready, 4 * i + j // 2 + 1)
                    dve.tensor_tensor(w_low[:, j // 2 % SLOTS, :], w[:, j // 2 % 2, :],
                                      w_high[:, j // 2 % SLOTS, :].bitcast(F32), ALU.subtract).then_inc(w_low_ready, 1)

            norm.vector(dve)
            def multiply(i, j):
                n = 8 * i + j
                dve.wait_ge(silu_ready, n + 1)
                dve.wait_ge(u_ready, n + 1)
                if not (start(i) and j < SLOTS):
                    dve.wait_ge(weighted_ready, n - SLOTS + 1)
                dve.tensor_tensor(hidden[:, j % SLOTS], silu_g[:, j % 2], aux[:, j % 2 * 2 + 1, :],
                                  ALU.mult).then_inc(hidden_ready, 1)

            split(0, 0)
            split(0, 2)
            multiply(0, 0)
            s = Steps(dve, small)
            wide = [P, NT, routed]

            def over(stat_ap):
                return stat_ap.unsqueeze(2).to_broadcast(wide)

            logits = acc[:, 0, 0:NT * routed].rearrange("p (t e) -> p t e", e=routed)
            if shared:
                dve.wait_ge(exp_ready, 1)
                s.then(dve.tensor_scalar(select[:], select[:], 1.0, None, ALU.add))
                s.then(dve.reciprocal(probs[:], select[:]))
                dve.wait_ge(router_in, 32)
                s.then(dve.tensor_tensor(select[:], probs[:], bias[:, :].unsqueeze(1).to_broadcast(wide), ALU.add))
            else:
                dve.wait_ge(logits_ready, 1)
                s.then(dve.tensor_reduce(stat[:], logits, AX, ALU.max))
                dve.tensor_tensor(select[:], logits, over(stat[:]), ALU.subtract).then_inc(shifted, 1)
                dve.wait_ge(exp_ready, 1)
                s.then(dve.tensor_reduce(stat[:], probs[:], AX, ALU.add))
                s.then(dve.reciprocal(stat[:], stat[:]))
                s.then(dve.tensor_tensor(probs[:], probs[:], over(stat[:]), ALU.mult))
                s.then(dve.tensor_copy(select[:], probs[:]))
            dve.wait_ge(iota_done, NT)
            for best in (first, second):
                s.then(dve.tensor_reduce(stat[:], select[:], AX, ALU.max))
                s.then(dve.tensor_tensor(rank[:], select[:], over(stat[:]), ALU.is_equal))
                s.then(dve.tensor_tensor(rank[:], rank[:], falling[:], ALU.mult))
                s.then(dve.tensor_reduce(stat[:], rank[:], AX, ALU.max))
                s.then(dve.tensor_tensor(best[:], rank[:], over(stat[:]), ALU.is_equal))
                if best is first:
                    s.then(dve.scalar_tensor_tensor(select[:], first[:], -BIG, select[:], ALU.mult, ALU.add))
            s.then(dve.tensor_tensor(first[:], first[:], second[:], ALU.add))
            s.then(dve.tensor_tensor(first[:], first[:], probs[:], ALU.mult))
            s.then(dve.tensor_reduce(stat[:], first[:], AX, ALU.add))
            s.then(dve.tensor_scalar(stat[:], stat[:], 1e-9 if shared else 1e-20, None, ALU.add))
            s.then(dve.reciprocal(stat[:], stat[:]))
            dve.tensor_tensor(comb[:, :, :], first[:], over(stat[:]), ALU.mult).then_inc(comb_ready, 1)


            def round_low(i, j):
                dve.wait_ge(high_ready, 8 * i + j + 1)
                dve.tensor_tensor(low[:, j % SLOTS], weighted[:, j % SLOTS], high[:, j % SLOTS].bitcast(F32),
                                  ALU.subtract).then_inc(low_ready, 1)

            pipeline(dve, 2 * E, [(3, multiply), (0, split), (4, round_low)], 8, 4, 2 * SLOTS)
            for q in range(4):
                dve.wait_ge(down_done, 2 * E - 1 + q // 2)
                dve.tensor_tensor(core.x[:, 2 * q:2 * q + 2, :], core.x[:, 2 * q:2 * q + 2, :],
                                  acc[:, q, :].rearrange("p (t d) -> p t d", t=2), ALU.add).then_inc(added, 1)

        @block.tensor
        def _(pe):
            norm.tensor(pe)
            def up(i, j):
                n = 8 * i + j
                s = j // 2 % SLOTS
                if j % 2 == 0:
                    pe.wait_ge(w_low_ready, 4 * i + j // 2 + 1)
                for g, ready in ((0, g_ready), (1, u_ready)):
                    if not (start(i) and j < 2):
                        pe.wait_ge(hidden_ready if g else silu_ready, n - 1)
                    for k in range(DC):
                        cols = slice(k * 2 * P + g * P, k * 2 * P + (g + 1) * P)
                        tokens = slice(j % 2 * HALF, (j % 2 + 1) * HALF)
                        for m, (a, b) in enumerate(three(w_high[:, s, cols], w_low[:, s, cols],
                                                         core.xnT_high[:, k, tokens], core.xnT_low[:, k, tokens])):
                            last = pe.matmul(aux[:, j % 2 * 2 + g, :], a, b, start=k + m == 0, stop=(k, m) == (DC - 1, 2))
                    last.then_inc(ready, 1)

            def down(i, j):
                s = j // 2 % SLOTS
                pe.wait_ge(low_ready, 8 * i + j + 1)
                for t in range(NT // 2):
                    tile = (j % 2) * (NT // 2) + t
                    cols = slice(t * P, (t + 1) * P)
                    for a, b in three(high[:, j % SLOTS, cols], low[:, j % SLOTS, cols], w_high[:, s, UP:], w_low[:, s, UP:]):
                        last = pe.matmul(acc[:, tile // 2, tile % 2 * D:(tile % 2 + 1) * D], a, b,
                                         start=False, stop=False, skip_group_check=True)
                last.then_inc(down_done, 1)

            pe.wait_ge(norm.low_ready, NT // 4)
            up(0, 0)
            pe.wait_ge(norm.low_ready, NT // 2)
            pe.wait_ge(norm.xnT_ready, NT // 2)
            pe.wait_ge(router_in, 32 if bias_dram is not None else 16)
            for t in range(NT):
                for k in range(DC):
                    last = pe.matmul(acc[:, 0, t * routed:(t + 1) * routed], core.xnT[:, k, t * P:(t + 1) * P],
                                     w_router[:, k, :], start=(k == 0), stop=(k == DC - 1))
            last.then_inc(logits_ready, 1)
            up(0, 1)
            up(0, 2)
            pe.wait_ge(comb_ready, 1)
            for t in range(NT):
                pe.transpose(acc[0:routed, 1 + t // 4, t % 4 * P:(t % 4 + 1) * P], comb[:, t, :],
                             core.ident[:, :]).then_inc(combT_turned, 1)
            pe.wait_ge(combT_ready, 2)
            for q in range(4):
                pe.matmul(acc[:, q, :], core.zeros[:, 0:P], core.zeros[:, :], start=True, stop=True,
                          skip_group_check=True)
            pipeline(pe, 2 * E, [(0, up), (SLOTS, down)], 8, 3, 2 * SLOTS)


HEADS, KV, HD = 32, 4, 128
GQ = HEADS // KV
STEPS = HEADS * NT
TILE_ORDER = [0, 7, 1, 6, 2, 5, 3, 4]
RMS_EPS = 1e-6


def gqa_layer(nc, core, wq_dram, wkv_dram, wo_dram, norm_w_dram, cos_dram, sin_dram):
    with ExitStack() as ctx:
        def sb(name, shape, dt=F32):
            return ctx.enter_context(nc.sbuf_tensor(f"gqa_{name}", shape, dt))

        sem = ctx.enter_context(Sems(nc, "gqa"))
        norm = Norm(nc, core, ctx, sem, "gqa", whole=False)
        k_scale = sb("k_scale", [P, KV, NT])
        w_q = sb("w_q", [P, 2, DC * HD])
        w_q_high = sb("w_q_high", [P, 2, DC * HD], F32R)
        w_q_low = sb("w_q_low", [P, 2, DC * HD], F32R)
        wo = sb("wo", [P, 4, D])
        norm_w = sb("norm_w", [P, 2])
        ones = sb("ones", [P, 1])
        below = sb("below", [P, P], BF16)
        ident_b = sb("ident_b", [P, P], BF16)
        square = sb("square", [P, 2, HALF])
        straight = sb("straight", [P, 2, HALF])
        turned_q = sb("turned_q", [P, 2, HALF])
        k_high = sb("k_high", [P, KV, T], F32R)
        k_low = sb("k_low", [P, KV, T], F32R)
        v = sb("v", [P, KV, NT, HD])
        q_high = sb("q_high", [P, 2, T], F32R)
        q_low = sb("q_low", [P, 2, T], F32R)
        mean_sq = sb("mean_sq", [P, 2, NT])
        q_scale = sb("q_scale", [P, 2, NT])
        probs = sb("probs", [P, 4, T])
        probsT = sb("probsT", [P, 4, T])
        neg_max = sb("neg_max", [P, 16])
        bias = sb("bias", [P, 16])
        row_sum = sb("row_sum", [P, 16])
        row_inv = sb("row_inv", [P, 16])
        oT = sb("oT", [P, 4, T])
        w_kv = probs[:, 2:4, :].rearrange("p a (b n) -> p (a b) n", b=2)
        w_kv_high = q_high[:, :, :].rearrange("p a (b n) -> p (a b) n", b=2)
        w_kv_low = q_low[:, :, :].rearrange("p a (b n) -> p (a b) n", b=2)
        k_tokens = oT[:, :, :].rearrange("p g (t d) -> p g t d", d=HD)
        cos_w = [probs[:, 0, :], core.xnT[:, 0, :]]
        sin_w = [probs[:, 1, :], core.xnT[:, 1, :]]

        tables_in = sem("tables_in")
        norm_w_in = sem("norm_w_in")
        made = sem("made")
        tables_ready = sem("tables_ready")
        w_kv_in = sem("w_kv_in")
        w_kv_high_ready = sem("w_kv_high_ready")
        w_kv_low_ready = sem("w_kv_low_ready")
        kv_done = sem("kv_done")
        k_copied = sem("k_copied")
        v_copied = sem("v_copied")
        k_squared = sem("k_squared")
        k_mean_ready = sem("k_mean_ready")
        k_scale_ready = sem("k_scale_ready")
        k_normed = sem("k_normed")
        k_turned = sem("k_turned")
        k_roped = sem("k_roped")
        k_ready = sem("k_ready")
        k_high_ready = sem("k_high_ready")
        k_low_ready = sem("k_low_ready")
        w_q_in = [sem("w_q_in0"), sem("w_q_in1")]
        wo_in = [sem("wo_in0"), sem("wo_in1")]
        w_q_high_ready = sem("w_q_high_ready")
        w_q_low_ready = sem("w_q_low_ready")
        projected = sem("projected")
        squared = sem("squared")
        roped = sem("roped")
        q_high_made = sem("q_high_made")
        q_summed = sem("q_summed")
        q_ready = sem("q_ready")
        square_sum = sem("square_sum")
        mean_ready = sem("mean_ready")
        q_scale_ready = sem("q_scale_ready")
        scored = sem("scored")
        max_ready = sem("max_ready")
        bias_ready = sem("bias_ready")
        exp_done = sem("exp_done")
        inv_ready = sem("inv_ready")
        wide_scaled = sem("wide_scaled")
        narrow_scaled = sem("narrow_scaled")
        chunk_turned = sem("chunk_turned")
        first_copied = sem("first_copied")
        rest_copied = sem("rest_copied")
        pv_done = sem("pv_done")
        oT_copied = sem("oT_copied")
        wo_done = sem("wo_done")
        added = sem("added")
        acc, aux = core.acc, core.aux

        TURN, WEIGH, OUT = 15, 18, 32
        def tile_of(j):
            return TILE_ORDER[j % NT]

        def wide(j):
            return tile_of(j) >= 4

        def width(j):
            return (tile_of(j) + 1) * P

        def flat(ap):
            return ap.rearrange("p a b -> p (a b)")

        def scores(j):
            return (flat(acc[:, 1:3, :]) if wide(j) else acc[:, 0, :])[:, 0:width(j)]

        def upto(value, total):
            return min(value, total) if isinstance(value, int) else value

        def turns(j):
            first = 3 * (j // 2)
            if not wide(j):
                return [(first % 2, 0, width(j), False)]
            return [((first + 1) % 2, 0, HALF, True), ((first + 2) % 2, HALF, width(j), False)]

        def wo_tile(i, j):
            if j % NT >= 4 or start(i) and j < NT:
                return None
            return j % NT + (0 if j // NT % 2 else 4)

        def wo_index(i, j):
            return NT * (2 * i + (j - NT) // (2 * NT)) + wo_tile(i, j)

        def steady(eng, stages, done=0):
            pipeline(eng, STEPS, stages, 32, done, lead=OUT + 3 * NT)

        block = ctx.enter_context(nc.Block())

        @block.sync
        def _(sp):
            def load_q(h, s):
                sp.dma_start(w_q[:, s, :], wq_dram[bass.ds(h, 1)].rearrange("a p k n -> (a p) (k n)")).then_inc(w_q_in[s], 16)

            def load_wo(h, s):
                sp.dma_start(wo[:, s, :], wo_dram[bass.ds(h, 1)].rearrange("a p n -> (a p) n")).then_inc(wo_in[s // 2], 16)

            sp.dma_start(w_kv, wkv_dram.rearrange("g p k n -> p g (k n)")).then_inc(w_kv_in, 16)
            sp.dma_start(norm_w[:, :], norm_w_dram).then_inc(norm_w_in, 16)
            for s in range(2):
                load_q(s, s)
            for s in range(4):
                load_wo(s, s)
            sp.wait_ge(norm.low_ready, NT // 2)
            sp.dma_start(core.xnT[:, 0, :], cos_dram).then_inc(tables_in, 16)
            sp.dma_start(core.xnT[:, 1, :], sin_dram).then_inc(tables_in, 16)

            def pair(i, s, q):
                for m in range(2):
                    if q:
                        sp.wait_ge(w_q_low_ready, 2 * i + m - 1)
                        load_q(2 * i + m, m)
                if not (isinstance(i, int) and i < 3):
                    sp.wait_ge(wo_done, NT * i - 2 * NT)
                    for m in range(2):
                        load_wo(2 * i - 2 + m, 2 * (1 - s) + m)

            pair(1, 1, True)
            pair(2, 0, True)
            pair(3, 1, True)
            with sp.Fori(2, HEADS // 4) as i:
                for s in range(2):
                    pair(2 * i + s, s, True)
            pair(HEADS // 2, 0, False)

        @block.gpsimd
        def _(pool):
            pool.memset(ones[:, :], 1.0).then_inc(made, 1)
            pool.memset(below[:, :], 0.0).then_inc(made, 1)
            pool.tensor_copy(ident_b[:, :], core.ident[:, :]).then_inc(made, 1)
            norm.gpsimd(pool)
            pool.wait_ge(made, 3)
            pool.affine_select(out=below[:, :], in_=below[:, :], compare_op=ALU.is_ge, fill=-BIG,
                               base=0, pattern=[[-1, P]], channel_multiplier=1).then_inc(made, 1)

            for n in range(KV + 2):
                if n < KV:
                    g = n
                    pool.wait_ge(k_mean_ready, g + 1)
                    pool.tensor_tensor(k_scale[:, g, :], k_scale[:, g, :], core.minus_half[:, :], ALU.pow).then_inc(k_scale_ready, 1)
                if n >= 2:
                    for c in range(2):
                        pool.wait_ge(k_roped, 2 * (n - 2) + c + 1)
                        pool.tensor_tensor(straight[:, c], straight[:, c], turned_q[:, c], ALU.add).then_inc(k_ready, 1)
            pool.wait_ge(k_low_ready, 2 * KV)

            def head(i, s):
                h = 2 * i + s
                if not start(i):
                    pool.wait_ge(scored, NT * h - NT)
                for c in range(2):
                    cols = slice(c * HALF, (c + 1) * HALF)
                    pool.wait_ge(roped, 2 * h + c + 1)
                    pool.tensor_tensor(q_high[:, s, cols], straight[:, c], turned_q[:, c], ALU.add).then_inc(q_high_made, 1)
                    pool.tensor_tensor(straight[:, c], straight[:, c], turned_q[:, c], ALU.add).then_inc(q_summed, 1)
                    pool.wait_ge(q_high_made, 2 * h + c + 1)
                    pool.wait_ge(q_summed, 2 * h + c + 1)
                    pool.tensor_tensor(q_low[:, s, cols], straight[:, c], q_high[:, s, cols].bitcast(F32), ALU.subtract).then_inc(q_ready, 1)
                pool.wait_ge(mean_ready, h + 1)
                pool.tensor_tensor(q_scale[:, s, :], mean_sq[:, s, :], core.minus_half[:, :], ALU.pow).then_inc(q_scale_ready, 1)

            for s in range(2):
                head(0, s)
            with pool.Fori(1, HEADS // 2) as i:
                for s in range(2):
                    head(i, s)

        @block.scalar
        def _(act):
            norm.scalar(act)

            act.wait_ge(w_kv_in, 16)
            for g in range(KV):
                act.activation(w_kv_high[:, g, :], w_kv[:, g, :], ACT.Copy).then_inc(w_kv_high_ready, 1)
            for g in range(KV):
                for q in range(4):
                    act.wait_ge(kv_done, 4 * g + q + 1)
                    bank = acc[:, q, :].rearrange("p (t w d) -> p t w d", w=2, d=HD)
                    for t in range(2):
                        act.activation(probsT[:, g, (2 * q + t) * HD:(2 * q + t + 1) * HD], bank[:, t, 0, :], ACT.Square,
                                       accum_out=k_scale[:, g, 2 * q + t:2 * q + t + 1]).then_inc(k_squared, 1)
                    act.activation(k_tokens[:, g, 2 * q:2 * q + 2, :], bank[:, :, 0, :], ACT.Copy).then_inc(k_copied, 1)
                    act.activation(v[:, g, 2 * q:2 * q + 2, :], bank[:, :, 1, :], ACT.Copy).then_inc(v_copied, 1)
            for g in range(KV):
                for c in range(2):
                    act.wait_ge(k_ready, 2 * g + c + 1)
                    act.activation(k_high[:, g, c * HALF:(c + 1) * HALF], straight[:, c], ACT.Copy).then_inc(k_high_ready, 1)

            def split(i, j):
                if j % NT == 0:
                    h = 4 * i + j // NT
                    s = j // NT % 2
                    act.wait_ge(w_q_in[s], 16 * (2 * i + j // (2 * NT)) + 16)
                    if not (start(i) and j < 2 * NT):
                        act.wait_ge(projected, 2 * h - 2)
                    act.activation(w_q_high[:, s, :], w_q[:, s, :], ACT.Copy).then_inc(w_q_high_ready, 1)

            def squares(i, j):
                if j % NT in (0, 2):
                    h = 4 * i + j // NT
                    c = j % NT // 2
                    act.wait_ge(projected, 2 * h + c + 1)
                    if not (start(i) and j < NT):
                        act.wait_ge(square_sum, h)
                    act.activation(square[:, c], acc[:, 3, :], ACT.Square).then_inc(squared, 1)

            def exp(i, j):
                act.wait_ge(bias_ready, 32 * i + j + 1)
                act.activation(probs[:, j % 4, 0:width(j)], scores(j), ACT.Exp, bias=bias[:, j % 16:j % 16 + 1],
                               scale=q_scale[:, j // NT % 2, tile_of(j):tile_of(j) + 1],
                               accum_out=row_sum[:, j % 16:j % 16 + 1]).then_inc(exp_done, 1)

            def scale_wide(i, j):
                if wide(j):
                    act.wait_ge(inv_ready, 32 * i + j + 1)
                    act.activation(probs[:, j % 4, 0:width(j)], probs[:, j % 4, 0:width(j)], ACT.Copy,
                                   scale=row_inv[:, j % 16:j % 16 + 1]).then_inc(wide_scaled, 1)

            def copy_first(i, j):
                for c, (bank, a, b, scalar) in enumerate(turns(j)):
                    if scalar:
                        act.wait_ge(chunk_turned, 48 * i + 3 * (j // 2) + 2)
                        act.activation(probsT[:, j % 4, a:b], aux[:, bank, 0:b - a], ACT.Copy).then_inc(first_copied, 1)

            def copy_oT(i, j):
                if j % NT >= NT - 2:
                    c = j % NT - (NT - 2)
                    act.wait_ge(pv_done, 32 * i + j + 1)
                    if not (start(i) and j < 4 * NT):
                        act.wait_ge(wo_done, NT * (2 * i + j // (2 * NT)) - NT)
                    act.activation(oT[:, j // NT % 4, c * HALF:(c + 1) * HALF], aux[:, 2 + c, :], ACT.Copy).then_inc(oT_copied, 1)

            steady(act, [(4, squares), (TURN, copy_first), (12, exp), (13, scale_wide), (WEIGH + 1, copy_oT), (0, split)])

        @block.vector
        def _(dve):
            norm.vector(dve)

            for g in range(KV):
                dve.wait_ge(w_kv_high_ready, g + 1)
                dve.tensor_tensor(w_kv_low[:, g, :], w_kv[:, g, :], w_kv_high[:, g, :].bitcast(F32), ALU.subtract).then_inc(w_kv_low_ready, 1)
            dve.wait_ge(norm_w_in, 16)
            dve.wait_ge(tables_in, 32)
            for kind in range(2):
                if kind == 1:
                    dve.wait_ge(tables_ready, 3)
                dve.tensor_scalar(cos_w[kind], core.xnT[:, 0, :], norm_w[:, kind:kind + 1], None, ALU.mult).then_inc(tables_ready, 1)
                dve.tensor_scalar(sin_w[kind][0:64, :], core.xnT[0:64, 1, :], norm_w[0:64, kind:kind + 1], None, ALU.mult).then_inc(tables_ready, 1)
                dve.tensor_scalar(sin_w[kind][64:128, :], core.xnT[64:128, 1, :], norm_w[64:128, kind:kind + 1], -1.0,
                                  ALU.mult, ALU.mult).then_inc(tables_ready, 1)
            dve.wait_ge(tables_ready, 6)

            def rotate(src, cols, kind, straight_out, turned_out, done):
                dve.tensor_tensor(straight_out, src, cos_w[kind][:, cols], ALU.mult)
                dve.tensor_tensor(turned_out[0:64], src[64:128], sin_w[kind][64:128, cols], ALU.mult)
                dve.tensor_tensor(turned_out[64:128], src[0:64], sin_w[kind][0:64, cols], ALU.mult).then_inc(done, 1)

            def k_part(m):
                g, c = m // 2, m % 2
                dve.wait_ge(k_high_ready, m + 1)
                dve.tensor_tensor(k_low[:, g, c * HALF:(c + 1) * HALF], straight[:, c], k_high[:, g, c * HALF:(c + 1) * HALF].bitcast(F32),
                                  ALU.subtract).then_inc(k_low_ready, 1)

            for n in range(KV + 2):
                if n < KV:
                    dve.wait_ge(k_squared, NT * n + NT)
                    dve.tensor_scalar(k_scale[:, n, :], k_scale[:, n, :], 1.0 / HD, RMS_EPS, ALU.mult, ALU.add).then_inc(k_mean_ready, 1)
                if 1 <= n < KV + 1:
                    g = n - 1
                    dve.wait_ge(k_scale_ready, g + 1)
                    dve.wait_ge(k_copied, 4 * g + 4)
                    dve.tensor_tensor(k_tokens[:, g], k_tokens[:, g], k_scale[:, g, :].unsqueeze(2).to_broadcast([P, NT, HD]),
                                      ALU.mult).then_inc(k_normed, 1)
                if n >= 2:
                    for c in range(2):
                        m = 2 * (n - 2) + c
                        dve.wait_ge(k_turned, m + 1)
                        if m >= 2:
                            dve.wait_ge(k_low_ready, m - 1)
                        rotate(aux[:, c, :], slice(c * HALF, (c + 1) * HALF), 0, straight[:, c], turned_q[:, c], k_roped)
                        if m >= 1:
                            k_part(m - 1)
            k_part(2 * KV - 1)

            def mean_square(i, j):
                if j % NT == 5:
                    h = 4 * i + j // NT
                    dve.wait_ge(square_sum, h + 1)
                    dve.tensor_scalar(mean_sq[:, j // NT % 2, :], acc[:, 0, 0:NT], RMS_EPS * HD, None, ALU.add).then_inc(mean_ready, 1)

            def row_max(i, j):
                n = 32 * i + j
                dve.wait_ge(scored, n + 1)
                dve.tensor_reduce(neg_max[:, j % 16:j % 16 + 1], scores(j), AX, ALU.max, negate=True).then_inc(max_ready, 1)
                if j % NT == 0:
                    dve.wait_ge(q_scale_ready, 4 * i + j // NT + 1)
                dve.wait_ge(max_ready, n + 1)
                dve.tensor_tensor(bias[:, j % 16:j % 16 + 1], neg_max[:, j % 16:j % 16 + 1],
                                  q_scale[:, j // NT % 2, tile_of(j):tile_of(j) + 1], ALU.mult).then_inc(bias_ready, 1)

            def normalise(i, j):
                n = 32 * i + j
                dve.wait_ge(exp_done, n + 1)
                dve.reciprocal(row_inv[:, j % 16:j % 16 + 1], row_sum[:, j % 16:j % 16 + 1]).then_inc(inv_ready, 1)
                if not wide(j):
                    dve.wait_ge(inv_ready, n + 1)
                    dve.tensor_scalar(probs[:, j % 4, 0:width(j)], probs[:, j % 4, 0:width(j)], row_inv[:, j % 16:j % 16 + 1],
                                      None, ALU.mult).then_inc(narrow_scaled, 1)

            def rope(i, j):
                if j % NT in (0, 2):
                    h = 4 * i + j // NT
                    c = j % NT // 2
                    dve.wait_ge(squared, 2 * h + c + 1)
                    if start(i) and j < NT:
                        dve.wait_ge(k_low_ready, 2 * KV)
                    else:
                        dve.wait_ge(q_ready, 2 * h + c - 1)
                    rotate(acc[:, 3, :], slice(c * HALF, (c + 1) * HALF), 1, straight[:, c], turned_q[:, c], roped)

            def copy_rest(i, j):
                for c, (bank, a, b, scalar) in enumerate(turns(j)):
                    if not scalar:
                        dve.wait_ge(chunk_turned, 48 * i + 3 * (j // 2) + (3 if wide(j) else 1))
                        dve.tensor_copy(probsT[:, j % 4, a:b], aux[:, bank, 0:b - a]).then_inc(rest_copied, 1)

            def add(i, j):
                t = wo_tile(i, j)
                if t is not None:
                    dve.wait_ge(wo_done, wo_index(i, j) + 1)
                    dve.tensor_tensor(core.x[:, t, :], core.x[:, t, :], acc[:, 3, 0:D], ALU.add).then_inc(added, 1)

            def split(i, j):
                if j % NT == 0:
                    s = j // NT % 2
                    dve.wait_ge(w_q_high_ready, 4 * i + j // NT + 1)
                    dve.tensor_tensor(w_q_low[:, s, :], w_q[:, s, :], w_q_high[:, s, :].bitcast(F32), ALU.subtract).then_inc(w_q_low_ready, 1)

            steady(dve, [(4, mean_square), (OUT + 1, add), (5, rope), (12, row_max), (13, normalise), (TURN, copy_rest), (0, split)])
            for t in range(4):
                add(STEPS // 32, t)

        @block.tensor
        def _(pe):
            norm.tensor(pe)
            pe.wait_ge(norm.low_ready, NT // 2)
            def kv(g):
                pe.wait_ge(w_kv_low_ready, g + 1)
                for t in range(NT):
                    if g >= 1 and t % 2 == 0:
                        pe.wait_ge(v_copied, 4 * g - 4 + t // 2 + 1)
                    for k in range(DC):
                        tokens = slice(t * P, (t + 1) * P)
                        cols = slice(k * 2 * HD, (k + 1) * 2 * HD)
                        for m, (a, b) in enumerate(three(core.xnT_high[:, k, tokens], core.xnT_low[:, k, tokens],
                                                         w_kv_high[:, g, cols], w_kv_low[:, g, cols])):
                            last = pe.matmul(acc[:, t // 2, t % 2 * 2 * HD:(t % 2 + 1) * 2 * HD], a, b,
                                             start=k + m == 0, stop=(k, m) == (DC - 1, 2))
                    if t % 2:
                        last.then_inc(kv_done, 1)

            def turn_k(g):
                pe.wait_ge(k_normed, g + 1)
                for c in range(2):
                    if g >= 1:
                        pe.wait_ge(k_roped, 2 * g + c - 1)
                    for t in range(4):
                        last = pe.transpose(aux[:, c, t * P:(t + 1) * P], k_tokens[:, g, 4 * c + t, :], core.ident[:, :])
                    last.then_inc(k_turned, 1)

            kv(0)
            kv(1)
            for g in range(2, KV):
                kv(g)
                turn_k(g - 2)
            turn_k(KV - 2)
            turn_k(KV - 1)
            pe.wait_ge(made, 4)
            pe.wait_ge(v_copied, 4 * KV)

            def project(i, j):
                if j % NT not in (0, 2):
                    return
                h = 4 * i + j // NT
                s = j // NT % 2
                c = j % NT // 2
                if c == 0:
                    pe.wait_ge(w_q_low_ready, h + 1)
                    if not (start(i) and j < OUT + NT):
                        pe.wait_ge(added, wo_index(i, j - OUT + 3) + 1)
                    elif j >= NT:
                        pe.wait_ge(roped, 2 * h)
                else:
                    pe.wait_ge(roped, 2 * h + 1)
                for k in range(DC):
                    for m, (a, b) in enumerate(three(w_q_high[:, s, k * HD:(k + 1) * HD], w_q_low[:, s, k * HD:(k + 1) * HD],
                                                     core.xnT_high[:, k, c * HALF:(c + 1) * HALF], core.xnT_low[:, k, c * HALF:(c + 1) * HALF])):
                        last = pe.matmul(acc[:, 3, :], a, b, start=k + m == 0, stop=(k, m) == (DC - 1, 2))
                last.then_inc(projected, 1)

            def sum_squares(i, j):
                if j % NT == 5:
                    pe.wait_ge(squared, 2 * (4 * i + j // NT) + 2)
                    if not (start(i) and j < NT):
                        pe.wait_ge(exp_done, 32 * i + j - 8)
                    for t in range(NT):
                        last = pe.matmul(acc[:, 0, t:t + 1], square[:, t // 4, t % 4 * P:(t % 4 + 1) * P], ones[:, :],
                                         start=True, stop=True)
                    last.then_inc(square_sum, 1)

            def score(i, j):
                n = 32 * i + j
                t = tile_of(j)
                s = j // NT % 2
                g = j // NT % KV
                if j % NT == 0:
                    pe.wait_ge(q_ready, 2 * (4 * i + j // NT) + 2)
                if start(i) and j < 2:
                    pe.wait_ge(k_low_ready, 2 * KV)
                    pe.wait_ge(mean_ready, 1)
                else:
                    pe.wait_ge(exp_done, n - 1)
                if j % NT == 6:
                    pe.wait_ge(mean_ready, upto(4 * i + j // NT + 2, HEADS))
                for a in range(0, width(j), HALF):
                    b = min(width(j), a + HALF)
                    for m, (left, right) in enumerate(three(q_high[:, s, t * P:(t + 1) * P], q_low[:, s, t * P:(t + 1) * P],
                                                            k_high[:, g, a:b], k_low[:, g, a:b])):
                        pe.matmul(scores(j)[:, a:b], left, right, start=m == 0, stop=m == 2 and b < width(j))
                pe.matmul(scores(j)[:, t * P:(t + 1) * P], ident_b[:, :], below[:, :], start=False, stop=True).then_inc(scored, 1)

            def turn(i, j):
                pair = 16 * i + j // 2
                first = start(i) and j < 2
                pe.wait_ge(wide_scaled if wide(j) else narrow_scaled, pair + 1)
                if first and not wide(j):
                    pe.wait_ge(k_roped, 2 * KV)
                for c, (bank, a, b, scalar) in enumerate(turns(j)):
                    if not first:
                        if not wide(j):
                            pe.wait_ge(first_copied, pair)
                        elif c == 0:
                            pe.wait_ge(rest_copied, 2 * pair)
                    if wide(j) and c == 1:
                        pe.wait_ge(rest_copied, 2 * pair + 1)
                    for s in range(a // P, b // P):
                        last = pe.transpose(aux[:, bank, s % 4 * P:(s % 4 + 1) * P],
                                            probs[:, j % 4, s * P:(s + 1) * P], core.ident[:, :])
                    last.then_inc(chunk_turned, 1)

            def weigh(i, j):
                t = tile_of(j)
                g = j // NT % KV
                pair = 16 * i + j // 2
                if j % NT < 2 and not (start(i) and j < NT):
                    pe.wait_ge(oT_copied, 2 * (4 * i + j // NT) - 1 + j % NT)
                if wide(j):
                    pe.wait_ge(first_copied, pair + 1)
                    pe.wait_ge(rest_copied, 2 * pair + 2)
                else:
                    pe.wait_ge(rest_copied, 2 * pair + 1)
                for s in range(t + 1):
                    last = pe.matmul(aux[:, 2 + t // 4, t % 4 * P:(t % 4 + 1) * P], v[:, g, s, :], probsT[:, j % 4, s * P:(s + 1) * P],
                                     start=(s == 0), stop=(s == t))
                last.then_inc(pv_done, 1)

            def out(i, j):
                t = wo_tile(i, j)
                if t is None:
                    return
                h = 4 * i + j // NT
                p = (j - NT) // (2 * NT)
                if t == 0:
                    pe.wait_ge(wo_in[p % 2], 32 * (i + p // 2) + 32)
                if j % NT == 0:
                    pe.wait_ge(oT_copied, 2 * h + 1 if t == 0 else 2 * h)
                    pe.wait_ge(roped, upto(2 * h + 2 * (OUT // NT), 2 * HEADS))
                if not (start(i) and wo_index(i, j) == 0):
                    pe.wait_ge(added, wo_index(i, j))
                for m in range(2):
                    slot = 2 * (p % 2) + m
                    last = pe.matmul(acc[:, 3, 0:D], oT[:, slot, t * P:(t + 1) * P], wo[:, slot, :], start=m == 0, stop=m == 1)
                last.then_inc(wo_done, 1)

            steady(pe, [(4, project), (4, sum_squares), (12, score), (OUT, out), (TURN, turn), (WEIGH, weigh)])
            for t in range(4):
                out(STEPS // 32, t)


H0, HD0 = 16, 16
STACK = 4 * HD0


def masked_attention_layer(nc, core, wq_dram, wk_dram, wv_dram, wo_dram):
    SCALE = 1.0 / T ** 0.5
    STEPS0 = H0 * NT
    SLOTS = 4
    HALVES = (0, 2, 1, 3)
    LOADS = 9
    with ExitStack() as ctx:
        def sb(name, shape, dt=F32):
            return ctx.enter_context(nc.sbuf_tensor(f"mat_{name}", shape, dt))

        sem = ctx.enter_context(Sems(nc, "mat"))
        norm = Norm(nc, core, ctx, sem, "mat", whole=False)
        w = sb("w", [P, DC, 3 * D])
        w_high = sb("w_high", [P, DC, 3 * D], F32R)
        w_low = sb("w_low", [P, DC, 3 * D], F32R)
        wo = sb("wo", [P, DC, D])
        ones = sb("ones", [P, P], F32R)
        after = sb("after", [P, P])
        below = sb("below", [P, P], BF16)
        below_k = sb("below_k", [P, P], BF16)
        ident_b = sb("ident_b", [P, P], BF16)
        top = sb("top", [P, NT])
        masked_keys = sb("masked_keys", [P, NT])
        v = sb("v", [P, NT, D])
        v_now = sb("v_now", [P, SLOTS, NT, HD0 + 1])
        v_later = sb("v_later", [P, NT, D])
        v_masked = sb("v_masked", [P, NT, D])
        high = sb("high", [P, 4, T], F32R)
        low = sb("low", [P, 4, T], F32R)
        qk = sb("qk", [P, SLOTS, 2, T], F32R)
        probsT = sb("probsT", [P, 4, T])
        neg_max = sb("neg_max", [P, SLOTS, NT])
        bound = sb("bound", [P, H0, NT], F32R)
        diag = sb("diag", [P, NT, P], F32R)
        weight = sb("weight", [P, NT, H0])
        outT_head = sb("outT_head", [P, 2, T])
        out = sb("out", [P, NT, H0, HD0 + 1])
        outT = sb("outT", [P, DC, T])

        made = sem("made")
        w_in = sem("w_in")
        w_high_ready = sem("w_high_ready")
        w_low_ready = sem("w_low_ready")
        wo_in = sem("wo_in")
        v_done = sem("v_done")
        v_ready = sem("v_ready")
        later_ready = sem("later_ready")
        v_masked_done = sem("v_masked_done")
        v_masked_ready = sem("v_masked_ready")
        projected = sem("projected")
        high_ready = sem("high_ready")
        low_ready = sem("low_ready")
        qk_in = [sem(f"qk_in{s}") for s in range(SLOTS)]
        scored = sem("scored")
        max_ready = sem("max_ready")
        bound_ready = sem("bound_ready")
        diag_ready = sem("diag_ready")
        max_spread = sem("max_spread")
        max_row_ready = sem("max_row_ready")
        key_scored = sem("key_scored")
        exp_done = sem("exp_done")
        v_now_ready = sem("v_now_ready")
        pv_done = sem("pv_done")
        outT_copied = sem("outT_copied")
        head_turned = sem("head_turned")
        out_copied = sem("out_copied")
        weight_ready = sem("weight_ready")
        weighted = sem("weighted")
        small = sem("small")
        out_ready = sem("out_ready")
        out_turned = sem("out_turned")
        outT_ready = sem("outT_ready")
        wo_done = sem("wo_done")
        added = sem("added")
        acc, aux = core.acc, core.aux

        def tile_of(j):
            return TILE_ORDER[j % NT]

        def flat(ap):
            return ap.rearrange("p a b -> p (a b)")

        def width(j):
            return (tile_of(j) + 1) * P

        def query_scores(j):
            return (flat(acc[:, 1:3, :]) if tile_of(j) >= 4 else acc[:, 0, :])[:, 0:width(j)]

        def key_width(j):
            return (NT - tile_of(j)) * P

        def key_scores(j):
            return (flat(aux[:, 0:2, :]) if tile_of(j) < 4 else acc[:, 3, :])[:, 0:key_width(j)]

        block = ctx.enter_context(nc.Block())

        @block.sync
        def _(sp):
            for n, w_dram in enumerate((wq_dram, wk_dram, wv_dram)):
                sp.dma_start(w[:, :, n * D:(n + 1) * D], w_dram).then_inc(w_in, 16)
            sp.dma_start(wo[:, :, :], wo_dram).then_inc(wo_in, 16)

            def copy(half, m):
                for w, order in ((0, (high, high, low, low)), (1, (high, low, high, low))):
                    for r, part in enumerate(order):
                        rows = part[m * HD0:(m + 1) * HD0, bass.ds(2 * w + half, 1), :].rearrange("p a t -> p (a t)")
                        sp.dma_start(qk[r * HD0:(r + 1) * HD0, m % SLOTS, w, :].bitcast(F32),
                                     rows.bitcast(F32)).then_inc(qk_in[m % SLOTS], 16)
                sp.dma_start(qk[STACK:STACK + 1, m % SLOTS, 0, :].bitcast(F32),
                             qk[STACK + 1:STACK + 2, m % SLOTS, 0, :].bitcast(F32)).then_inc(qk_in[m % SLOTS], 16)

            sp.wait_ge(made, 14)
            sp.wait_ge(low_ready, 2)
            for m in range(SLOTS):
                copy(0, m)
            for m in range(SLOTS, H0 // 2):
                sp.wait_ge(key_scored, NT * (m - SLOTS + 1))
                copy(0, m)
            sp.wait_ge(low_ready, 4)
            with sp.Fori(1, 2) as half:
                for m in range(H0 // 2):
                    sp.wait_ge(key_scored, STEPS0 // 2 * half + NT * (m - SLOTS + 1))
                    copy(half, m)

        @block.gpsimd
        def _(pool):
            pool.memset(ones[:, :].bitcast(F32), 1.0).then_inc(made, 1)
            pool.memset(after[:, :], 0.0).then_inc(made, 1)
            pool.memset(below[:, :], 0.0).then_inc(made, 1)
            pool.memset(below_k[:, :], 0.0).then_inc(made, 1)
            pool.memset(top[:, :], 0.0).then_inc(made, 1)
            pool.iota(masked_keys[:, :], [[-P, NT]], base=T - 1, channel_multiplier=-1,
                      allow_small_or_imprecise_dtypes=True).then_inc(made, 1)
            pool.tensor_copy(ident_b[:, :], core.ident[:, :]).then_inc(made, 1)
            pool.memset(v_now[:, :, :, HD0:HD0 + 1], 1.0).then_inc(made, 1)
            norm.gpsimd(pool)
            pool.wait_ge(made, 8)
            pool.affine_select(out=after[:, :], in_=after[:, :], compare_op=ALU.is_ge, fill=1.0,
                               base=0, pattern=[[1, P]], channel_multiplier=-1).then_inc(made, 1)
            pool.affine_select(out=below[:, :], in_=below[:, :], compare_op=ALU.is_ge, fill=-BIG,
                               base=0, pattern=[[-1, P]], channel_multiplier=1).then_inc(made, 1)
            pool.affine_select(out=below_k[:, :], in_=below_k[:, :], compare_op=ALU.is_ge, fill=-BIG,
                               base=0, pattern=[[1, P]], channel_multiplier=-1).then_inc(made, 1)
            pool.affine_select(out=top[:, :], in_=top[:, :], compare_op=ALU.not_equal, fill=BIG,
                               base=-(T - 1), pattern=[[P, NT]], channel_multiplier=1).then_inc(made, 1)
            pool.wait_ge(made, 12)
            pool.memset(qk[STACK:P, :, :, :].bitcast(F32), 0.0).then_inc(made, 1)
            pool.wait_ge(made, 13)
            pool.memset(qk[STACK:STACK + 1, :, 1, :].bitcast(F32), 1.0).then_inc(made, 1)
            pool.wait_ge(made, 14)
            pool.memset(outT_head[:, :, :], 0.0).then_inc(made, 1)
            pool.memset(v_later[:, NT - 1, :], 0.0).then_inc(later_ready, 1)
            pool.wait_ge(v_ready, 4)
            for t in range(NT - 2, -1, -1):
                pool.wait_ge(later_ready, NT - 1 - t)
                pool.tensor_tensor(v_later[:, t, :], v_later[:, t + 1, :], v[:, t + 1, :], ALU.add).then_inc(later_ready, 1)

            def prepare(i, s):
                h = SLOTS * i + s
                pool.wait_ge(bound_ready, h + 1)
                if not (start(i) and s == 0):
                    pool.wait_ge(max_spread, 2 * h)
                pool.tensor_tensor(diag[:, :, :], core.ident[:, :].unsqueeze(1).to_broadcast([P, NT, P]),
                                   bound[:, bass.ds(h, 1), :].rearrange("p a t -> p (a t)").bitcast(F32).unsqueeze(2).to_broadcast([P, NT, P]),
                                   ALU.mult).then_inc(diag_ready, 1)
                if not start(i):
                    pool.wait_ge(pv_done, NT * (h - SLOTS + 1))
                pool.tensor_copy(v_now[:, s, :, 0:HD0], v[:, :, bass.ds(HD0 * h, HD0)]).then_inc(v_now_ready, 1)

            for s in range(SLOTS):
                prepare(0, s)
            with pool.Fori(1, H0 // SLOTS) as i:
                for s in range(SLOTS):
                    prepare(i, s)
            pool.wait_ge(weight_ready, 2)
            for q in range(4):
                v_m = v_masked[:, 2 * q:2 * q + 2, :].rearrange("p t (h d) -> p t h d", d=HD0)
                pool.tensor_tensor(v_m, v_m, weight[:, 2 * q:2 * q + 2, :].unsqueeze(3).to_broadcast([P, 2, H0, HD0]),
                                   ALU.mult).then_inc(weighted, 1)

        @block.scalar
        def _(act):
            act.wait_ge(w_in, 48)
            for k in range(DC):
                act.activation(w_high[:, k, :], w[:, k, :], ACT.Copy).then_inc(w_high_ready, 1)
            norm.scalar(act)
            for n, m in enumerate(HALVES):
                act.wait_ge(projected, n + 1)
                act.activation(high[:, m, :], flat(acc[:, 2 * (n % 2):2 * (n % 2) + 2, :]), ACT.Copy).then_inc(high_ready, 1)
            for q in range(4):
                act.wait_ge(v_done, q + 1)
                act.activation(v[:, 2 * q:2 * q + 2, :], aux[:, q, :].rearrange("p (t d) -> p t d", t=2), ACT.Copy).then_inc(v_ready, 1)

            for n, q in enumerate(range(3, -1, -1)):
                act.wait_ge(v_masked_done, n + 1)
                act.activation(v_masked[:, 2 * q:2 * q + 2, :], aux[:, q, :].rearrange("p (t d) -> p t d", t=2),
                               ACT.Copy).then_inc(v_masked_ready, 1)

            def exp(i, j):
                n = 32 * i + j
                act.wait_ge(key_scored, n + 1)
                if not (start(i) and j < 4):
                    act.wait_ge(pv_done, n - 3)
                act.activation(probsT[:, j % 4, 0:key_width(j)], key_scores(j), ACT.Exp, scale=SCALE).then_inc(exp_done, 1)

            def copy_outT(i, j):
                if j % NT >= NT - 2:
                    c = j % NT - (NT - 2)
                    act.wait_ge(pv_done, 32 * i + j + 1)
                    if not (start(i) and j < 2 * NT):
                        act.wait_ge(head_turned, 4 * i + j // NT - 1)
                    act.activation(outT_head[0:HD0 + 1, j // NT % 2, c * HALF:(c + 1) * HALF], aux[0:HD0 + 1, 2 + c, :],
                                   ACT.Copy).then_inc(outT_copied, 1)

            def copy_out(i, j):
                if j % NT == NT - 1:
                    act.wait_ge(head_turned, 4 * i + j // NT + 1)
                    act.activation(out[:, :, bass.ds(4 * i + j // NT, 1), :].rearrange("p t h d -> p t (h d)"),
                                   acc[:, 3, 0:NT * (HD0 + 1)].rearrange("p (t d) -> p t d", d=HD0 + 1),
                                   ACT.Copy).then_inc(out_copied, 1)

            act.wait_ge(made, 15)
            pipeline(act, STEPS0, [(2, copy_outT), (0, exp), (5, copy_out)], 32, lead=3 * NT)
            act.wait_ge(weight_ready, 1)
            act.activation(weight[:, :, :], weight[:, :, :], ACT.Exp, scale=SCALE).then_inc(weight_ready, 1)
            for q in range(4):
                act.wait_ge(out_turned, q + 1)
                act.activation(outT[:, :, 2 * q * P:(2 * q + 2) * P],
                               acc[:, q, :].rearrange("p (k t) -> p k t", k=DC), ACT.Copy).then_inc(outT_ready, 1)

        @block.vector
        def _(dve):
            norm.vector(dve)
            for k in range(DC):
                dve.wait_ge(w_high_ready, k + 1)
                dve.tensor_tensor(w_low[:, k, :], w[:, k, :], w_high[:, k, :].bitcast(F32), ALU.subtract).then_inc(w_low_ready, 1)
            for n, m in enumerate(HALVES):
                dve.wait_ge(high_ready, n + 1)
                dve.tensor_tensor(low[:, m, :], flat(acc[:, 2 * (n % 2):2 * (n % 2) + 2, :]), high[:, m, :].bitcast(F32),
                                  ALU.subtract).then_inc(low_ready, 1)
            def row_max(i, j):
                n = 32 * i + j
                t = tile_of(j)
                s = j // NT % SLOTS
                dve.wait_ge(scored, n + 1)
                dve.tensor_reduce(neg_max[:, s, t:t + 1], query_scores(j), AX, ALU.max, negate=True).then_inc(max_ready, 1)
                if j % NT == NT - 1:
                    dve.wait_ge(max_ready, n + 1)
                    dve.tensor_tensor(bound[:, bass.ds(4 * i + j // NT, 1), :].rearrange("p a t -> p (a t)"),
                                      neg_max[:, s, :], top[:, :], ALU.min).then_inc(bound_ready, 1)

            def max_row(c):
                def stage(i, j):
                    if j % NT == NT - 1:
                        dve.wait_ge(max_spread, 8 * i + 2 * (j // NT) + c + 1)
                        dve.tensor_copy(qk[STACK:STACK + 1, j // NT % SLOTS, 0, c * HALF:(c + 1) * HALF],
                                        acc[STACK:STACK + 1, 0, :]).then_inc(max_row_ready, 1)
                return stage

            dve.wait_ge(made, 12)
            pipeline(dve, STEPS0, [(4, max_row(0)), (6, max_row(1)), (0, row_max)], 32, lead=3 * NT)
            s = Steps(dve, small)
            dve.tensor_scalar(weight[:, :, :], bound[:, :, :].bitcast(F32).rearrange("p h t -> p t h"), 0.0, None, ALU.min).then_inc(weight_ready, 1)
            dve.wait_ge(weight_ready, 2)
            wide = [P, NT, H0]
            row_sum = out[:, :, :, HD0:HD0 + 1].rearrange("p t h a -> p t (h a)")
            dve.wait_ge(weighted, 4)
            s.then(dve.tensor_tensor(weight[:, :, :], weight[:, :, :], masked_keys[:, :].unsqueeze(2).to_broadcast(wide), ALU.mult))
            dve.wait_ge(out_copied, H0)
            s.then(dve.tensor_tensor(weight[:, :, :], row_sum, weight[:, :, :], ALU.add))
            s.then(dve.reciprocal(weight[:, :, :], weight[:, :, :]))
            for q in range(4):
                two = slice(2 * q, 2 * q + 2)
                v_m = v_masked[:, two, :].rearrange("p t (h d) -> p t h d", d=HD0)
                s.then(dve.tensor_tensor(v_m, v_m, out[:, two, :, 0:HD0], ALU.add))
                dve.tensor_tensor(v_m, v_m, weight[:, two, :].unsqueeze(3).to_broadcast([P, 2, H0, HD0]),
                                  ALU.mult).then_inc(out_ready, 1)
            for t in range(NT):
                dve.wait_ge(wo_done, t + 1)
                dve.tensor_tensor(core.x[:, t, :], core.x[:, t, :], aux[:, t % 4, 0:D], ALU.add).then_inc(added, 1)

        @block.tensor
        def _(pe):
            norm.tensor(pe)
            pe.wait_ge(norm.low_ready, NT // 2)
            pe.wait_ge(w_low_ready, DC)
            for n, m in enumerate(HALVES):
                if n >= 2:
                    pe.wait_ge(low_ready, n - 1)
                for h in range(2):
                    for k in range(DC):
                        cols = slice(m * P, (m + 1) * P)
                        tokens = slice(h * HALF, (h + 1) * HALF)
                        for c, (a, b) in enumerate(three(w_high[:, k, cols], w_low[:, k, cols],
                                                         core.xnT_high[:, k, tokens], core.xnT_low[:, k, tokens])):
                            last = pe.matmul(acc[:, 2 * (n % 2) + h, :], a, b, start=k + c == 0, stop=(k, c) == (DC - 1, 2))
                last.then_inc(projected, 1)
            for t in range(NT):
                for k in range(DC):
                    tokens = slice(t * P, (t + 1) * P)
                    for c, (a, b) in enumerate(three(core.xnT_high[:, k, tokens], core.xnT_low[:, k, tokens],
                                                     w_high[:, k, 2 * D:], w_low[:, k, 2 * D:])):
                        last = pe.matmul(aux[:, t // 2, t % 2 * D:(t % 2 + 1) * D], a, b, start=k + c == 0, stop=(k, c) == (DC - 1, 2))
                if t % 2:
                    last.then_inc(v_done, 1)
            pe.wait_ge(made, 14)
            pe.wait_ge(low_ready, 4)

            def sum_masked(tiles):
                for t in tiles:
                    pe.wait_ge(later_ready, NT - t)
                    out_t = aux[:, t // 2, t % 2 * D:(t % 2 + 1) * D]
                    pe.matmul(out_t, after[:, :], v[:, t, :], start=True, stop=False)
                    last = pe.matmul(out_t, ones[:, :].bitcast(F32), v_later[:, t, :], start=False, stop=True)
                    if t % 2 == 0:
                        last.then_inc(v_masked_done, 1)

            def score(i, j):
                t = tile_of(j)
                s = j // NT % SLOTS
                if j % NT == 0:
                    pe.wait_ge(qk_in[s], 16 * LOADS * (i + j // 32) + 16 * LOADS)
                if not (start(i) and j < 2):
                    pe.wait_ge(max_ready, 32 * i + j - 1)
                if j % NT in (4, 6) and not (start(i) and j < NT):
                    pe.wait_ge(max_row_ready, 8 * i + 2 * (j // NT) - 1 + (j % NT - 4) // 2)
                for a in range(0, width(j), HALF):
                    b = min(width(j), a + HALF)
                    pe.matmul(query_scores(j)[:, a:b], qk[:, s, 0, t * P:(t + 1) * P], qk[:, s, 1, a:b],
                              start=True, stop=b < width(j))
                pe.matmul(query_scores(j)[:, t * P:(t + 1) * P], ident_b[:, :], below[:, :],
                          start=False, stop=True).then_inc(scored, 1)

            def spread(c, lag):
                def stage(i, j):
                    if j % NT == NT - 1:
                        pe.wait_ge(diag_ready, 4 * i + j // NT + 1)
                        now = 32 * i + j + lag
                        pe.wait_ge(max_ready, min(now, STEPS0) if isinstance(i, int) else now)
                        if c == 1:
                            pe.wait_ge(max_row_ready, 8 * i + 2 * (j // NT) + 1)
                        pe.matmul(acc[:, 0, :], ones[:, :], flat(diag[:, :, :])[:, c * HALF:(c + 1) * HALF],
                                  start=True, stop=True).then_inc(max_spread, 1)
                return stage

            def score_keys(i, j):
                b = tile_of(j)
                s = j // NT % SLOTS
                if j % NT == 0:
                    pe.wait_ge(max_row_ready, 8 * i + 2 * (j // NT) + 2)
                if start(i) and j < 2:
                    pe.wait_ge(v_masked_ready, 4)
                else:
                    pe.wait_ge(exp_done, 32 * i + j - 1)
                if j % NT == 5 and not (start(i) and j < NT):
                    pe.wait_ge(out_copied, 4 * i + j // NT)
                for a in range(0, key_width(j), HALF):
                    z = min(key_width(j), a + HALF)
                    pe.matmul(key_scores(j)[:, a:z], qk[:, s, 1, b * P:(b + 1) * P], qk[:, s, 0, b * P + a:b * P + z],
                              start=True, stop=a > 0)
                pe.matmul(key_scores(j)[:, 0:P], ident_b[:, :], below_k[:, :], start=False, stop=True).then_inc(key_scored, 1)

            def weigh(i, j):
                b = tile_of(j)
                if j % NT == 0:
                    pe.wait_ge(v_now_ready, 4 * i + j // NT + 1)
                pe.wait_ge(exp_done, 32 * i + j + 1)
                for c in range(b // 4, 2):
                    if j % NT == 0 and not (start(i) and j < NT):
                        pe.wait_ge(outT_copied, 8 * i + 2 * (j // NT) - 1 + c)
                    lo = max(b * P, c * HALF)
                    last = pe.matmul(aux[0:HD0 + 1, 2 + c, lo - c * HALF:HALF],
                                     v_now[:, j // NT % SLOTS, b, :],
                                     probsT[:, j % 4, lo - b * P:(c + 1) * HALF - b * P],
                                     start=b == 0, stop=b == 4 * c + 3 if c == 0 else b == 4, skip_group_check=True)
                last.then_inc(pv_done, 1)

            def turn_head(i, j):
                if j % NT == NT - 1:
                    h = 4 * i + j // NT
                    pe.wait_ge(outT_copied, 2 * h + 2)
                    now = 32 * i + j + 5
                    pe.wait_ge(exp_done, min(now, STEPS0) if isinstance(i, int) else now)
                    pe.matmul(acc[:, 3, 0:NT * (HD0 + 1)], core.zeros[:, 0:P], core.zeros[:, 0:NT * (HD0 + 1)], start=True, stop=True)
                    for t in range(NT):
                        last = pe.transpose(acc[:, 3, t * (HD0 + 1):(t + 1) * (HD0 + 1)],
                                            outT_head[0:HD0 + 1, j // NT % 2, t * P:(t + 1) * P], core.ident[0:HD0 + 1, 0:HD0 + 1])
                    last.then_inc(head_turned, 1)

            pe.wait_ge(v_ready, 4)
            for n in range(NT):
                score(0, n)
                if n % 4 == 3:
                    sum_masked(range(NT - n // 4 * 4 - 1, NT - n // 4 * 4 - 5, -1))
            pipeline(pe, STEPS0, [(4, spread(0, 4)), (6, spread(1, 6)), (0, score), (19, turn_head), (14, score_keys), (16, weigh)],
                     32, NT, 3 * NT)
            pe.wait_ge(wo_in, 16)
            for q in range(NT // 2):
                pe.wait_ge(out_ready, q + 1)
                for t in (2 * q, 2 * q + 1):
                    for k in range(DC):
                        last = pe.transpose(acc[:, q, (2 * k + t % 2) * P:(2 * k + t % 2 + 1) * P],
                                            v_masked[:, t, k * P:(k + 1) * P], core.ident[:, :])
                last.then_inc(out_turned, 1)
            for t in range(NT):
                pe.wait_ge(outT_ready, t // 2 + 1)
                if t >= 4:
                    pe.wait_ge(added, t - 3)
                for k in range(DC):
                    last = pe.matmul(aux[:, t % 4, 0:D], outT[:, k, t * P:(t + 1) * P], wo[:, k, :],
                                     start=(k == 0), stop=(k == DC - 1))
                last.then_inc(wo_done, 1)


INNER, TAPS = 512, 4
NC = INNER // P


def conv_layer(nc, core, in_dram, out_dram, channel_dram):
    with ExitStack() as ctx:
        def sb(name, shape, dt=F32):
            return ctx.enter_context(nc.sbuf_tensor(f"conv_{name}", shape, dt))

        sem = ctx.enter_context(Sems(nc, "conv"))
        norm = Norm(nc, core, ctx, sem, "conv", whole=False)
        w_in = sb("w_in", [P, NC, DC, 2 * P])
        w_in_high = sb("w_in_high", [P, NC, DC, 2 * P], F32R)
        w_in_low = sb("w_in_low", [P, NC, DC, 2 * P], F32R)
        w_out = sb("w_out", [P, NC, D])
        channel = sb("channel", [P, NC, TAPS + 2])
        xi = sb("xi", [P, 2, TAPS - 1 + T])
        conv = sb("conv", [P, 2, T])
        gate = sb("gate", [P, 2, T])
        hidden = sb("hidden", [P, 2, T])

        w_in_in = sem("w_in_in")
        w_out_in = sem("w_out_in")
        channel_in = sem("channel_in")
        padded = sem("padded")
        w_high_ready = sem("w_high_ready")
        w_low_ready = sem("w_low_ready")
        xi_done = sem("xi_done")
        xi_ready = sem("xi_ready")
        gate_done = sem("gate_done")
        gate_ready = sem("gate_ready")
        tap = sem("tap")
        conv_ready = sem("conv_ready")
        silu_ready = sem("silu_ready")
        hidden_ready = sem("hidden_ready")
        out_done = sem("out_done")
        added = sem("added")
        acc, aux = core.acc, core.aux
        block = ctx.enter_context(nc.Block())

        @block.sync
        def _(sp):
            sp.dma_start(channel[:, :, :], channel_dram).then_inc(channel_in, 16)
            sp.dma_start(w_in[:, :, :, :], in_dram.rearrange("f p k n -> p f k n")).then_inc(w_in_in, 16)
            sp.dma_start(w_out[:, :, :], out_dram.rearrange("f p n -> p f n")).then_inc(w_out_in, 16)

        @block.gpsimd
        def _(pool):
            pool.memset(xi[:, :, 0:TAPS - 1], 0.0).then_inc(padded, 1)
            norm.gpsimd(pool)

        @block.scalar
        def _(act):
            norm.scalar(act)
            act.wait_ge(w_in_in, 16)
            for f in range(NC):
                act.activation(w_in_high[:, f], w_in[:, f], ACT.Copy).then_inc(w_high_ready, 1)
            for f in range(NC + 1):
                if f < NC:
                    act.wait_ge(xi_done, f + 1)
                    if f >= 2:
                        act.wait_ge(conv_ready, f - 1)
                    act.activation(xi[:, f % 2, TAPS - 1:], aux[:, 0:2, :].rearrange("p a b -> p (a b)"),
                                   ACT.Copy).then_inc(xi_ready, 1)
                    act.wait_ge(gate_done, f + 1)
                    if f >= 2:
                        act.wait_ge(hidden_ready, f - 1)
                    act.activation(gate[:, f % 2], aux[:, 2:4, :].rearrange("p a b -> p (a b)"),
                                   ACT.Silu).then_inc(gate_ready, 1)
                if f >= 1:
                    r = f - 1
                    act.wait_ge(conv_ready, r + 1)
                    act.activation(conv[:, r % 2], conv[:, r % 2], ACT.Silu,
                                   bias=channel[:, r, TAPS:TAPS + 1]).then_inc(silu_ready, 1)

        @block.vector
        def _(dve):
            norm.vector(dve)
            for f in range(NC):
                dve.wait_ge(w_high_ready, f + 1)
                dve.tensor_tensor(w_in_low[:, f], w_in[:, f], w_in_high[:, f].bitcast(F32), ALU.subtract).then_inc(w_low_ready, 1)
            dve.wait_ge(padded, 1)
            dve.wait_ge(channel_in, 16)
            for f in range(NC + 1):
                if f < NC:
                    dve.wait_ge(xi_ready, f + 1)
                    if f >= 2:
                        dve.wait_ge(hidden_ready, f - 1)
                    dve.tensor_scalar(conv[:, f % 2], xi[:, f % 2, 0:T], channel[:, f, 0:1], None, ALU.mult).then_inc(tap, 1)
                    for k in range(1, TAPS):
                        dve.wait_ge(tap, (TAPS - 1) * f + k)
                        dve.scalar_tensor_tensor(conv[:, f % 2], xi[:, f % 2, k:k + T], channel[:, f, k:k + 1],
                                                 conv[:, f % 2], ALU.mult, ALU.add).then_inc(tap if k < TAPS - 1 else conv_ready, 1)
                if f >= 1:
                    r = f - 1
                    dve.wait_ge(silu_ready, r + 1)
                    dve.wait_ge(gate_ready, r + 1)
                    if r >= 2:
                        dve.wait_ge(out_done, r - 1)
                    dve.scalar_tensor_tensor(hidden[:, r % 2], conv[:, r % 2], channel[:, r, TAPS + 1:TAPS + 2],
                                             gate[:, r % 2], ALU.mult, ALU.mult).then_inc(hidden_ready, 1)
            dve.wait_ge(out_done, NC)
            for q in range(4):
                dve.tensor_tensor(core.x[:, 2 * q:2 * q + 2, :], core.x[:, 2 * q:2 * q + 2, :],
                                  acc[:, q, :].rearrange("p (t d) -> p t d", t=2), ALU.add).then_inc(added, 1)

        @block.tensor
        def _(pe):
            norm.tensor(pe)
            pe.wait_ge(norm.low_ready, NT // 2)
            for q in range(4):
                pe.matmul(acc[:, q, :], core.zeros[:, 0:P], core.zeros[:, :], start=True, stop=True, skip_group_check=True)
            pe.wait_ge(w_out_in, 16)
            for f in range(NC + 2):
                if f < NC:
                    pe.wait_ge(w_low_ready, f + 1)
                    for w, done, read in ((0, xi_done, xi_ready), (1, gate_done, gate_ready)):
                        if f >= 1:
                            pe.wait_ge(read, f)
                        for h in range(2):
                            for k in range(DC):
                                tokens = slice(h * HALF, (h + 1) * HALF)
                                for m, (a, b) in enumerate(three(w_in_high[:, f, k, w * P:(w + 1) * P], w_in_low[:, f, k, w * P:(w + 1) * P],
                                                                 core.xnT_high[:, k, tokens], core.xnT_low[:, k, tokens])):
                                    last = pe.matmul(aux[:, 2 * w + h, :], a, b, start=k + m == 0, stop=(k, m) == (DC - 1, 2))
                        last.then_inc(done, 1)
                if f >= 2:
                    r = f - 2
                    pe.wait_ge(hidden_ready, r + 1)
                    for t in range(NT):
                        last = pe.matmul(acc[:, t // 2, t % 2 * D:(t % 2 + 1) * D], hidden[:, r % 2, t * P:(t + 1) * P],
                                         w_out[:, r, :], start=False, stop=False, skip_group_check=True)
                    last.then_inc(out_done, 1)


STATE, RANK = 16, 128


def scan_layer(nc, core, in_dram, bc_dram, dt_dram, channel_dram, a_log_dram):
    with ExitStack() as ctx:
        def sb(name, shape, dt=F32):
            return ctx.enter_context(nc.sbuf_tensor(f"scan_{name}", shape, dt))

        sem = ctx.enter_context(Sems(nc, "scan"))
        norm = Norm(nc, core, ctx, sem, "scan")
        ROWS = 2 * STATE
        w_delta = sb("w_delta", [P, DC, RANK])
        w_bc = sb("w_bc", [P, DC, ROWS])
        w_dt = sb("w_dt", [P, DC, P])
        channel = sb("channel", [P, DC, 2])
        a = sb("a", [P, DC, STATE])
        pick = sb("pick", [P, ROWS, P], BF16)
        low = sb("low", [P, T])
        parts = sb("parts", [P, T], BF16)
        rest = sb("rest", [ROWS, 2, T])
        part32 = sb("part32", [ROWS, 2, T])
        z = sb("z", [P, DC, T])
        delta = sb("delta", [P, DC, T])
        du = sb("du", [P, DC, T])
        b_all = sb("b_all", [P, 4, T])
        decay = sb("decay", [P, 4, T])
        dbu = sb("dbu", [P, 4, T])
        h = sb("h", [P, 4, T])
        hc = sb("hc", [P, 4, T])

        w_in = sem("w_in")
        channel_in = sem("channel_in")
        made = sem("made")
        a_ready = sem("a_ready")
        low_done = sem("low_done")
        low_ready = sem("low_ready")
        bc_done = sem("bc_done")
        split = sem("split")
        parts_ready = sem("parts_ready")
        dt_done = sem("dt_done")
        abs_ready = sem("abs_ready")
        soft = sem("soft")
        log_ready = sem("log_ready")
        relu_ready = sem("relu_ready")
        delta_ready = sem("delta_ready")
        du_ready = sem("du_ready")
        b_spread = sem("b_spread")
        c_spread = sem("c_spread")
        b_ready = sem("b_ready")
        decay_ready = sem("decay_ready")
        dbu_ready = sem("dbu_ready")
        h_ready = sem("h_ready")
        hc_ready = sem("hc_ready")
        summed = sem("summed")
        y_ready = sem("y_ready")
        y_turned = sem("y_turned")
        added = sem("added")
        acc, aux = core.acc, core.aux
        block = ctx.enter_context(nc.Block())

        @block.sync
        def _(sp):
            for dst, src in ((w_delta, in_dram), (w_bc, bc_dram), (w_dt, dt_dram)):
                sp.dma_start(dst[:, :, :], src).then_inc(w_in, 16)
            for dst, src in ((channel, channel_dram), (a, a_log_dram)):
                sp.dma_start(dst[:, :, :], src).then_inc(channel_in, 16)

        @block.gpsimd
        def _(pool):
            norm.gpsimd(pool)
            pool.wait_ge(norm.rstd_ready, NT // 2)
            pool.memset(pick[:, :, :], 0.0).then_inc(made, 1)
            pool.wait_ge(made, 1)
            pool.memset(parts[96:128, :], 0.0).then_inc(made, 1)
            for q in range(3):
                pool.wait_ge(made, q + 2)
                pool.affine_select(out=pick[32 * q:32 * q + 32, :, :], in_=pick[32 * q:32 * q + 32, :, :],
                                   compare_op=ALU.not_equal, fill=1.0, base=0,
                                   pattern=[[-1, ROWS], [0, P]], channel_multiplier=1).then_inc(made, 1)
            pool.wait_ge(made, 5)
            for k in range(DC):
                pool.wait_ge(delta_ready, k + 1)
                pool.tensor_tensor(du[:, k], delta[:, k], core.xnT[:, k], ALU.mult).then_inc(du_ready, 1)
            pool.wait_ge(du_ready, DC)

            def multiply(i, j):
                n = 4 * i + j
                pool.wait_ge(b_ready, n + 1)
                if not (start(i) and j < 2):
                    pool.wait_ge(h_ready, 2 * n - 2)
                for k in range(DC):
                    pool.tensor_tensor(dbu[:, 2 * (j % 2) + k], du[:, k], b_all[:, j % 4], ALU.mult).then_inc(dbu_ready, 1)

            pipeline(pool, STATE, [(0, multiply)], 4, lead=8)

        @block.scalar
        def _(act):
            norm.scalar(act)
            act.wait_ge(low_done, 1)
            act.activation(low[:, :], acc[:, 0:2, :].rearrange("p a b -> p (a b)"), ACT.Copy).then_inc(low_ready, 1)
            act.wait_ge(channel_in, 32)
            act.activation(a[:, :, :], a[:, :, :], ACT.Exp).then_inc(a_ready, 1)
            for k in range(DC):
                act.wait_ge(dt_done, k + 1)
                act.activation(z[:, k], acc[:, 2 * k:2 * k + 2, :].rearrange("p a b -> p (a b)"), ACT.Abs,
                               bias=channel[:, k, 0:1]).then_inc(abs_ready, 1)
            for k in range(DC):
                act.wait_ge(abs_ready, k + 1)
                act.activation(z[:, k], z[:, k], ACT.Exp, scale=-1.0).then_inc(soft, 1)
            for k in range(DC):
                act.wait_ge(soft, k + 1)
                act.activation(z[:, k], z[:, k], ACT.Ln, bias=1.0).then_inc(log_ready, 1)
            act.wait_ge(delta_ready, DC)
            act.wait_ge(a_ready, 2)

            def copy_b(i, j):
                n = 4 * i + j
                act.wait_ge(b_spread, n + 1)
                if not (start(i) and j < 4):
                    act.wait_ge(dbu_ready, 2 * n - 6)
                act.activation(b_all[:, j % 4], aux[:, 0:2, :].rearrange("p a b -> p (a b)"), ACT.Copy).then_inc(b_ready, 1)

            def make_decay(i, j):
                n = 4 * i + j
                if not (start(i) and j < 2):
                    act.wait_ge(h_ready, 2 * n - 2)
                for k in range(DC):
                    act.activation(decay[:, 2 * (j % 2) + k], delta[:, k], ACT.Exp,
                                   scale=a[:, k, bass.ds(n, 1)]).then_inc(decay_ready, 1)

            pipeline(act, STATE, [(0, copy_b), (1, make_decay)], 4, lead=8)

        @block.vector
        def _(dve):
            norm.vector(dve)
            dve.wait_ge(a_ready, 1)
            dve.tensor_scalar(a[:, :, :], a[:, :, :], -1.0, None, ALU.mult).then_inc(a_ready, 1)
            dve.wait_ge(bc_done, 1)
            bc = aux[0:ROWS, 0:2, :].rearrange("p a b -> p (a b)")
            s = Steps(dve, split)
            s.then(dve.tensor_copy(parts[0:32, :], bc))
            s.then(dve.tensor_copy(part32[:, 0], parts[0:32, :]))
            s.then(dve.tensor_tensor(rest[:, 0], bc, part32[:, 0], ALU.subtract))
            s.then(dve.tensor_copy(parts[32:64, :], rest[:, 0]))
            s.then(dve.tensor_copy(part32[:, 1], parts[32:64, :]))
            s.then(dve.tensor_tensor(rest[:, 1], rest[:, 0], part32[:, 1], ALU.subtract))
            dve.tensor_copy(parts[64:96, :], rest[:, 1]).then_inc(parts_ready, 1)
            for k in range(DC):
                dve.wait_ge(abs_ready, k + 1)
                dve.tensor_scalar(delta[:, k], acc[:, 2 * k:2 * k + 2, :].rearrange("p a b -> p (a b)"),
                                  channel[:, k, 0:1], 0.0, ALU.add, ALU.max).then_inc(relu_ready, 1)
            for k in range(DC):
                dve.wait_ge(log_ready, k + 1)
                dve.wait_ge(relu_ready, k + 1)
                dve.tensor_tensor(delta[:, k], delta[:, k], z[:, k], ALU.add).then_inc(delta_ready, 1)

            def scan(i, j):
                n = 4 * i + j
                c_all = aux[:, 2:4, :].rearrange("p a b -> p (a b)")
                for k in range(DC):
                    m = 2 * (j % 2) + k
                    if not (start(i) and j < 2):
                        dve.wait_ge(hc_ready, 2 * n - 3 + k)
                    dve.wait_ge(decay_ready, 2 * n + k + 1)
                    dve.wait_ge(dbu_ready, 2 * n + k + 1)
                    dve.tensor_tensor_scan(h[:, m], decay[:, m], dbu[:, m], 0.0, ALU.mult, ALU.add).then_inc(h_ready, 1)
                dve.wait_ge(c_spread, n + 1)
                for k in range(DC):
                    m = 2 * (j % 2) + k
                    if not (start(i) and j < 2):
                        dve.wait_ge(summed, 2 * n - 3 + k)
                    dve.wait_ge(h_ready, 2 * n + k + 1)
                    dve.tensor_tensor(hc[:, m], h[:, m], c_all, ALU.mult).then_inc(hc_ready, 1)

            pipeline(dve, STATE, [(0, scan)], 4, lead=8)
            dve.wait_ge(summed, STATE * DC)
            for k in range(DC):
                dve.scalar_tensor_tensor(z[:, k], core.xnT[:, k], channel[:, k, 1:2],
                                         acc[:, 2 * k:2 * k + 2, :].rearrange("p a b -> p (a b)"),
                                         ALU.mult, ALU.add).then_inc(y_ready, 1)
            for q in range(4):
                dve.wait_ge(y_turned, q + 1)
                dve.tensor_tensor(core.x[:, 2 * q:2 * q + 2, :], core.x[:, 2 * q:2 * q + 2, :],
                                  aux[:, q, :].rearrange("p (t d) -> p t d", t=2), ALU.add).then_inc(added, 1)

        @block.tensor
        def _(pe):
            norm.tensor(pe)
            pe.wait_ge(norm.xnT_ready, NT // 2)
            pe.wait_ge(w_in, 48)

            def project(out, w, rhs, chunks):
                for hf in range(2):
                    for k in range(chunks):
                        last = pe.matmul(out[:, hf, :], w(k), rhs(k)[:, hf * HALF:(hf + 1) * HALF],
                                         start=(k == 0), stop=(k == chunks - 1))
                return last

            project(acc[:, 0:2, :], lambda k: w_delta[:, k, :], lambda k: core.xnT[:, k], DC).then_inc(low_done, 1)
            project(aux[0:ROWS, 0:2, :], lambda k: w_bc[:, k, :], lambda k: core.xnT[:, k], DC).then_inc(bc_done, 1)
            pe.wait_ge(low_ready, 1)
            for k in range(DC):
                project(acc[:, 2 * k:2 * k + 2, :], lambda _: w_dt[:, k, :], lambda _: low, 1).then_inc(dt_done, 1)
            pe.wait_ge(parts_ready, 1)
            pe.wait_ge(made, 5)
            pe.wait_ge(relu_ready, DC)
            for q in range(4):
                pe.matmul(acc[:, q, :], core.zeros[:, 0:P], core.zeros[:, :], start=True, stop=True, skip_group_check=True)

            def spread(bank, row, done):
                for hf in range(2):
                    last = pe.matmul(aux[:, bank + hf, :], pick[:, bass.ds(row, 1), :].rearrange("p a m -> p (a m)"),
                                     parts[:, hf * HALF:(hf + 1) * HALF], start=True, stop=True)
                last.then_inc(done, 1)

            def spread_b(i, j):
                if not (start(i) and j < 1):
                    pe.wait_ge(b_ready, 4 * i + j)
                spread(0, 4 * i + j, b_spread)

            def spread_c(i, j):
                if not (start(i) and j < 1):
                    pe.wait_ge(hc_ready, 2 * (4 * i + j))
                spread(2, STATE + 4 * i + j, c_spread)

            def sums(i, j):
                for k in range(DC):
                    pe.wait_ge(hc_ready, 2 * (4 * i + j) + k + 1)
                    for hf in range(2):
                        last = pe.matmul(acc[:, 2 * k + hf, :], core.ident[:, :], hc[:, 2 * (j % 2) + k, hf * HALF:(hf + 1) * HALF],
                                         start=False, stop=False, skip_group_check=True)
                    last.then_inc(summed, 1)

            pipeline(pe, STATE, [(0, spread_b), (1, spread_c), (2, sums)], 4, lead=8)
            for q in range(NT // 2):
                pe.wait_ge(y_ready, DC)
                for t in (2 * q, 2 * q + 1):
                    for k in range(DC):
                        last = pe.transpose(aux[:, q, (t % 2) * D + k * P:(t % 2) * D + (k + 1) * P],
                                            z[:, k, t * P:(t + 1) * P], core.ident[:, :])
                last.then_inc(y_turned, 1)


def store(nc, core, out_dram):
    with ExitStack() as ctx:
        stored = ctx.enter_context(nc.semaphore("stored"))
        block = ctx.enter_context(nc.Block())

        @block.sync
        def _(sp):
            sp.dma_start(out_dram.rearrange("(n p) d -> p n d", p=P), core.x[:, :, :]).then_inc(stored, 16)
            sp.wait_ge(stored, 16)


def build(nc, a, out_dram):
    comb_dram = nc.dram_tensor("comb_by_expert", (E, T), F32, kind="Internal").ap()
    with ExitStack() as ctx:
        core = Core(nc, ctx)
        constants(nc, core, a["x"])
        masked_attention_layer(nc, core, a["a0_wq"], a["a0_wk"], a["a0_wv"], a["a0_wo"])
        ffn_layer(nc, core, "f1", a["f0_up"], a["f0_down"], a["f0_router"], a["f0_bias"], comb_dram, 8)
        conv_layer(nc, core, a["c_in"], a["c_out"], a["c_channel"])
        ffn_layer(nc, core, "f2", a["f0_up"], a["f0_down"], a["f0_router"], a["f0_bias"], comb_dram, 8)
        scan_layer(nc, core, a["s_in"], a["s_bc"], a["s_dt"], a["s_channel"], a["s_a_log"])
        ffn_layer(nc, core, "f3", a["f1_up"], a["f1_down"], a["f1_router"], None, comb_dram, 0)
        gqa_layer(nc, core, a["g_wq"], a["g_wkv"], a["g_wo"], a["g_norm_w"], a["cos"], a["sin"])
        ffn_layer(nc, core, "f4", a["f1_up"], a["f1_down"], a["f1_router"], None, comb_dram, 0)
        store(nc, core, out_dram)


def layouts(inputs):
    import numpy as np

    i = {k: np.asarray(v) for k, v in inputs.items()}

    def rows(w):
        return w.reshape(-1, P, w.shape[-1]).transpose(1, 0, 2)

    def blocks(w, n):
        return w.reshape(DC, P, n, -1).transpose(2, 1, 0, 3)

    a = {"x": i["L0_attn_a_x"].reshape(T, D)}
    for name in ("q", "k", "v", "o"):
        a[f"a0_w{name}"] = rows(i[f"L0_attn_a_W{name}"])
    w12 = i["L0_ffn_w12"]
    gates = np.concatenate([i["L0_ffn_sw1"].reshape(8, P, D), w12[:, :P]])
    ups = np.concatenate([i["L0_ffn_sw2"].reshape(8, P, D), w12[:, P:]])
    both = np.concatenate([gates, ups], 1).transpose(0, 2, 1)
    a["f0_up"] = both.reshape(E, DC, P, 2 * P).transpose(0, 2, 1, 3)
    a["f0_down"] = np.concatenate([i["L0_ffn_sw3"].T.reshape(8, P, D), i["L0_ffn_w3"].transpose(0, 2, 1)])
    a["f0_router"] = rows(i["L0_ffn_router_w"].T)
    a["f0_bias"] = i["L0_ffn_expert_bias"]
    w_in = i["L0_attn_b_w_in"].reshape(2, NC, P, DC, P)
    a["c_in"] = w_in.transpose(1, 4, 3, 0, 2).reshape(NC, P, DC, 2 * P)
    a["c_out"] = i["L0_attn_b_w_out"].T.reshape(NC, P, D)
    channel = np.concatenate([i["L0_attn_b_conv_w"][:, 0], i["L0_attn_b_conv_b"][:, None], i["L0_attn_b_D"][:, None]], 1)
    a["c_channel"] = rows(channel)
    x_proj = i["L1_attn_a_x_proj_w"].T
    a["s_in"], a["s_bc"] = rows(x_proj[:, :RANK]), rows(x_proj[:, RANK:])
    a["s_dt"] = i["L1_attn_a_dt_proj_w"].T.reshape(RANK, DC, P)
    a["s_channel"] = rows(np.stack([i["L1_attn_a_dt_proj_b"], i["L1_attn_a_D"]], 1))
    a["s_a_log"] = rows(i["L1_attn_a_A_log"])
    both = np.concatenate([i["L1_ffn_wg"], i["L1_ffn_wu"]], 2)
    a["f1_up"] = both.reshape(E, DC, P, 2 * P).transpose(0, 2, 1, 3)
    a["f1_down"] = i["L1_ffn_wd"]
    a["f1_router"] = rows(i["L1_ffn_gate_w"].T)
    heads = [GQ * (n % KV) + n // KV for n in range(HEADS)]
    a["g_wq"] = blocks(i["L1_attn_b_Wq"], HEADS)[heads]
    a["g_wkv"] = np.concatenate([blocks(i["L1_attn_b_Wk"], KV), blocks(i["L1_attn_b_Wv"], KV)], 3)
    a["g_wo"] = i["L1_attn_b_Wo"].reshape(HEADS, HD, D)[heads]
    a["g_norm_w"] = np.stack([i["L1_attn_b_k_norm_w"], i["L1_attn_b_q_norm_w"]], 1)
    inv_freq = (1.0 / np.float32(1000000.0) ** (np.arange(0, HD, 2, dtype=np.float32) / np.float32(HD))).astype(np.float32)
    angle = np.outer(np.concatenate([inv_freq, inv_freq]), np.arange(T, dtype=np.float32)).astype(np.float32)
    a["cos"], a["sin"] = np.cos(angle), np.sin(angle)
    return {k: np.ascontiguousarray(v) for k, v in a.items()}


def kernel(**inputs):
    import numpy as np
    import concourse.bacc as bacc
    from concourse.bass_utils import run_bass_kernel_spmd

    nc = bacc.Bacc("TRN2", target_bir_lowering=False, num_devices=1)
    arrays, aps = {}, {}
    for name, array in layouts(inputs).items():
        arrays[f"in_{name}"] = array
        aps[name] = nc.dram_tensor(f"in_{name}", array.shape, mybir.dt.from_np(array.dtype), kind="ExternalInput").ap()
    out = nc.dram_tensor("out_stream", (T, D), F32, kind="ExternalOutput").ap()
    build(nc, aps, out)
    result = run_bass_kernel_spmd(nc, [arrays], core_ids=[0])
    return np.asarray(result.results[0]["out_stream"]).reshape(1, T, D)
```
